# Optimizing a Trainium2 kernel written in Bass

```python
import numpy as np
import jax
import jax.numpy as jnp

def _softmax(x, axis=-1):
    return jax.nn.softmax(x, axis=axis)

def _gelu(x):
    return jax.nn.gelu(x, approximate=True)

def _silu(x):
    return jax.nn.silu(x)

def _sigmoid(x):
    return jax.nn.sigmoid(x)

def _layernorm(x, axis=-1, eps=1e-05):
    m = jnp.mean(x, axis=axis, keepdims=True)
    v = jnp.var(x, axis=axis, keepdims=True)
    return (x - m) / jnp.sqrt(v + eps)

def _scatter_add(tgt, idx, src, axis=0):
    return tgt.at[idx].add(src)

def _segment_sum(src, seg, n):
    return jax.ops.segment_sum(src, seg, n)
kernel_name = 'mk_vit_tower_d1_tok_img768_r4_ace310'

def setup_inputs(seed: int=0):
    np.random.seed(seed)
    _w = jnp.asarray

    def _rec_inputs():
        import jax
        import jax.numpy as jnp
        _rk = jax.random.key(seed)
        x = -0.000356955 + 1 * jax.random.normal(jax.random.fold_in(_rk, 1), (16, 3, 96, 96), jnp.float32)
        return x
    x = _rec_inputs()

    def _L0_tok_setup():
        import jax, jax.numpy as jnp
        import numpy as np
        DCT_P = 8
        PATCH = 16

        def _dct_matrix(N: int) -> jnp.ndarray:
            n = jnp.arange(N, dtype=jnp.float32)
            D = jnp.sqrt(2.0 / N) * jnp.cos(jnp.pi * (2.0 * n[None, :] + 1.0) * n[:, None] / (2.0 * N))
            return D.at[0].mul(1.0 / jnp.sqrt(2.0))
        key = jax.random.key(seed)
        kx, kw, kb = jax.random.split(key, 3)
        x = jax.random.normal(kx, (128, 3, 224, 224), dtype=jnp.float32)
        w = jax.random.normal(kw, (192, 3, PATCH, PATCH), dtype=jnp.float32) * 0.02
        b = jax.random.normal(kb, (192,), dtype=jnp.float32) * 0.02
        return {'x': x, 'w': w, 'b': b}
    _L0_tok_all = _L0_tok_setup()
    _L0_tok_in = {k: v for k, v in _L0_tok_all.items() if k in ('w', 'b')}
    del _L0_tok_all

    def _L0_attn_setup():
        import jax, jax.numpy as jnp
        import numpy as np
        N_STATE = 192
        N_HEAD = 12
        D_HEAD = N_STATE // N_HEAD
        M_SLOTS = 100

        def _split_heads(t):
            B, T, _ = t.shape
            return t.reshape(B, T, N_HEAD, D_HEAD).transpose(0, 2, 1, 3)

        def _merge_heads(t):
            B, H, T, D = t.shape
            return t.transpose(0, 2, 1, 3).reshape(B, T, H * D)

        def _attn(q, k, v):
            w = jax.nn.softmax(jnp.einsum('bhqd,bhkd->bhqk', q, k), axis=-1)
            return jnp.einsum('bhqk,bhkd->bhqd', w, v)
        key = jax.random.key(seed)
        ks = jax.random.split(key, 10)
        B, S = (2, 512)
        sc = 0.02
        return {'x': jax.random.normal(ks[0], (B, S, N_STATE), dtype=jnp.float32), 'w_attn': jax.random.normal(ks[1], (N_STATE, 3 * N_STATE), dtype=jnp.float32) * sc, 'b_attn': jnp.zeros((3 * N_STATE,), dtype=jnp.float32), 'w_proj': jax.random.normal(ks[2], (N_STATE, N_STATE), dtype=jnp.float32) * sc, 'b_proj': jnp.zeros((N_STATE,), dtype=jnp.float32), 'w_mem': jax.random.normal(ks[3], (N_STATE, 2 * N_STATE), dtype=jnp.float32) * sc, 'b_mem': jnp.zeros((2 * N_STATE,), dtype=jnp.float32), 'w_alpha': jax.random.normal(ks[4], (2 * N_STATE, N_STATE), dtype=jnp.float32) * sc, 'b_alpha': jnp.zeros((N_STATE,), dtype=jnp.float32), 'memory_features': jax.random.normal(ks[5], (1, M_SLOTS, N_STATE), dtype=jnp.float32) * sc}
    _L0_attn_all = _L0_attn_setup()
    _L0_attn_in = {k: v for k, v in _L0_attn_all.items() if k in ('w_attn', 'b_attn', 'w_proj', 'b_proj', 'w_mem', 'b_mem', 'w_alpha', 'b_alpha', 'memory_features')}
    del _L0_attn_all

    def _L0_ffn_setup():
        import jax, jax.numpy as jnp
        import numpy as np
        EPS_NORM = 1e-05
        RMS_EPS = 1e-05

        def _l2_normalize(v):
            n = jnp.sqrt(jnp.sum(v * v, axis=-1, keepdims=True))
            return v / jnp.maximum(n, EPS_NORM)

        def _rms_norm(x, weight, eps):
            ms = jnp.mean(x * x, axis=-1, keepdims=True)
            return x * jax.lax.rsqrt(ms + eps) * weight
        key = jax.random.key(seed)
        ks = jax.random.split(key, 6)
        B, T, D = (8, 1024, 192)
        S, F = (64, 768)
        x = jax.random.normal(ks[0], (B, T, D), dtype=jnp.float32)
        slots = 0.02 * jax.random.normal(ks[1], (S, D), dtype=jnp.float32)
        scale = jnp.ones((S,), dtype=jnp.float32)
        fc1_weight = 0.02 * jax.random.normal(ks[2], (S, D, F), dtype=jnp.float32)
        fc1_bias = jnp.zeros((S, F), dtype=jnp.float32)
        fc2_weight = 0.02 * jax.random.normal(ks[3], (S, F, D), dtype=jnp.float32)
        fc2_bias = jnp.zeros((S, D), dtype=jnp.float32)
        norm_weight = jnp.ones((D,), dtype=jnp.float32)
        return {'x': x, 'slots': slots, 'scale': scale, 'fc1_weight': fc1_weight, 'fc1_bias': fc1_bias, 'fc2_weight': fc2_weight, 'fc2_bias': fc2_bias, 'norm_weight': norm_weight}
    _L0_ffn_all = _L0_ffn_setup()
    _L0_ffn_in = {k: v for k, v in _L0_ffn_all.items() if k in ('slots', 'scale', 'fc1_weight', 'fc1_bias', 'fc2_weight', 'fc2_bias', 'norm_weight')}
    del _L0_ffn_all
    return {'x': x, 'L0_tok_w': _L0_tok_in['w'], 'L0_tok_b': _L0_tok_in['b'], 'L0_attn_w_attn': _L0_attn_in['w_attn'], 'L0_attn_b_attn': _L0_attn_in['b_attn'], 'L0_attn_w_proj': _L0_attn_in['w_proj'], 'L0_attn_b_proj': _L0_attn_in['b_proj'], 'L0_attn_w_mem': _L0_attn_in['w_mem'], 'L0_attn_b_mem': _L0_attn_in['b_mem'], 'L0_attn_w_alpha': _L0_attn_in['w_alpha'], 'L0_attn_b_alpha': _L0_attn_in['b_alpha'], 'L0_attn_memory_features': _L0_attn_in['memory_features'], 'L0_ffn_slots': _L0_ffn_in['slots'], 'L0_ffn_scale': _L0_ffn_in['scale'], 'L0_ffn_fc1_weight': _L0_ffn_in['fc1_weight'], 'L0_ffn_fc1_bias': _L0_ffn_in['fc1_bias'], 'L0_ffn_fc2_weight': _L0_ffn_in['fc2_weight'], 'L0_ffn_fc2_bias': _L0_ffn_in['fc2_bias'], 'L0_ffn_norm_weight': _L0_ffn_in['norm_weight']}

def reference(x, L0_tok_w, L0_tok_b, L0_attn_w_attn, L0_attn_b_attn, L0_attn_w_proj, L0_attn_b_proj, L0_attn_w_mem, L0_attn_b_mem, L0_attn_w_alpha, L0_attn_b_alpha, L0_attn_memory_features, L0_ffn_slots, L0_ffn_scale, L0_ffn_fc1_weight, L0_ffn_fc1_bias, L0_ffn_fc2_weight, L0_ffn_fc2_bias, L0_ffn_norm_weight):
    import jax
    import jax.numpy as jnp

    def _L0_tok_ref(x, w, b):
        import jax, jax.numpy as jnp
        import numpy as np
        DCT_P = 8
        PATCH = 16

        def _dct_matrix(N: int) -> jnp.ndarray:
            n = jnp.arange(N, dtype=jnp.float32)
            D = jnp.sqrt(2.0 / N) * jnp.cos(jnp.pi * (2.0 * n[None, :] + 1.0) * n[:, None] / (2.0 * N))
            return D.at[0].mul(1.0 / jnp.sqrt(2.0))
        B, C, H, W = x.shape
        P = DCT_P
        D = _dct_matrix(P).astype(x.dtype)
        xb = x.reshape(B, C, H // P, P, W // P, P)
        xd = jnp.einsum('uk,bcikjl,vl->bciujv', D, xb, D)
        xd = xd.reshape(B, C, H, W)
        y = jax.lax.conv_general_dilated(xd, w, window_strides=(PATCH, PATCH), padding='VALID', dimension_numbers=('NCHW', 'OIHW', 'NCHW'))
        y = y + b[None, :, None, None]
        y = y.reshape(B, y.shape[1], -1).transpose(0, 2, 1)
        return y

    def _L0_attn_ref(x, w_attn, b_attn, w_proj, b_proj, w_mem, b_mem, w_alpha, b_alpha, memory_features):
        import jax, jax.numpy as jnp
        import numpy as np
        N_STATE = 192
        N_HEAD = 12
        D_HEAD = N_STATE // N_HEAD
        M_SLOTS = 100

        def _split_heads(t):
            B, T, _ = t.shape
            return t.reshape(B, T, N_HEAD, D_HEAD).transpose(0, 2, 1, 3)

        def _merge_heads(t):
            B, H, T, D = t.shape
            return t.transpose(0, 2, 1, 3).reshape(B, T, H * D)

        def _attn(q, k, v):
            w = jax.nn.softmax(jnp.einsum('bhqd,bhkd->bhqk', q, k), axis=-1)
            return jnp.einsum('bhqk,bhkd->bhqd', w, v)
        B, S, _ = x.shape
        qkv = x @ w_attn + b_attn
        q, k, v = jnp.split(qkv, 3, axis=-1)
        q = _split_heads(q)
        k = _split_heads(k)
        v = _split_heads(v)
        a = _merge_heads(_attn(q, k, v))
        mem = jnp.broadcast_to(memory_features, (B, M_SLOTS, N_STATE))
        mkv = mem @ w_mem + b_mem
        mk, mv = jnp.split(mkv, 2, axis=-1)
        mk = _split_heads(mk)
        mv = _split_heads(mv)
        a1 = _merge_heads(_attn(q, mk, mv))
        alpha = jax.nn.sigmoid(jnp.concatenate([a, a1], axis=-1) @ w_alpha + b_alpha)
        fused = alpha * a + (1.0 - alpha) * a1
        return fused @ w_proj + b_proj

    def _L0_ffn_ref(x, slots, scale, fc1_weight, fc1_bias, fc2_weight, fc2_bias, norm_weight):
        import jax, jax.numpy as jnp
        import numpy as np
        EPS_NORM = 1e-05
        RMS_EPS = 1e-05

        def _l2_normalize(v):
            n = jnp.sqrt(jnp.sum(v * v, axis=-1, keepdims=True))
            return v / jnp.maximum(n, EPS_NORM)

        def _rms_norm(x, weight, eps):
            ms = jnp.mean(x * x, axis=-1, keepdims=True)
            return x * jax.lax.rsqrt(ms + eps) * weight
        xn = _rms_norm(x, norm_weight, RMS_EPS)
        tok = _l2_normalize(xn)
        sl = _l2_normalize(slots) * scale[:, None]
        logits = jnp.einsum('sd,btd->bst', sl, tok)
        dispatch_w = jax.nn.softmax(logits, axis=-1)
        combine_w = jax.nn.softmax(logits, axis=-2)
        y = jnp.einsum('btd,bst->bsd', xn, dispatch_w)
        y = jnp.einsum('sio,bsi->bso', fc1_weight, y) + fc1_bias
        y = jax.nn.gelu(y, approximate=False)
        y = jnp.einsum('sio,bsi->bso', fc2_weight, y) + fc2_bias
        out = jnp.einsum('bsd,bst->btd', y, combine_w)
        return out
    h = _L0_tok_ref(x, L0_tok_w, L0_tok_b)
    h = h + _L0_attn_ref(_layernorm(h, axis=-1), L0_attn_w_attn, L0_attn_b_attn, L0_attn_w_proj, L0_attn_b_proj, L0_attn_w_mem, L0_attn_b_mem, L0_attn_w_alpha, L0_attn_b_alpha, L0_attn_memory_features)
    h = h + _L0_ffn_ref(_layernorm(h, axis=-1), L0_ffn_slots, L0_ffn_scale, L0_ffn_fc1_weight, L0_ffn_fc1_bias, L0_ffn_fc2_weight, L0_ffn_fc2_bias, L0_ffn_norm_weight)
    return h

_drawn_inputs = setup_inputs


def setup_inputs(seed=0):
    import zlib

    import numpy as np

    out = dict(_drawn_inputs(seed))
    spreads = {'L0_attn_b_attn': (0.0, 0.303),
     'L0_attn_b_proj': (0.0, 0.1),
     'L0_attn_b_mem': (0.0, 0.374),
     'L0_attn_b_alpha': (0.0, 0.8),
     'L0_ffn_scale': (1.0, 0.6),
     'L0_ffn_fc1_bias': (0.0, 0.8),
     'L0_ffn_fc2_bias': (0.0, 0.394),
     'L0_ffn_norm_weight': (1.0, 0.6)}
    factors = {'L0_attn_w_attn': 4.714,
     'L0_attn_w_mem': 8.0,
     'L0_attn_w_alpha': 8.0,
     'L0_attn_memory_features': 8.0,
     'L0_ffn_slots': 8.0,
     'L0_ffn_fc1_weight': 8.0,
     'L0_ffn_fc2_weight': 7.503}
    for name, (base, spread) in spreads.items():
        noise = np.random.default_rng([zlib.crc32(name.encode()), seed]).standard_normal(out[name].shape)
        drawn = base * np.exp(spread * noise) if base else spread * noise
        out[name] = jnp.asarray(drawn.astype(out[name].dtype))
    for name, factor in factors.items():
        out[name] = (out[name] * factor).astype(out[name].dtype)
    return out
```

```python
from contextlib import ExitStack

import numpy as np

import concourse.bass as bass
from concourse import mybir

F32 = mybir.dt.float32
ALU = mybir.AluOpType
ACT = mybir.ActivationFunctionType
AX = mybir.AxisListType

B, T, D = 16, 36, 192
NTOK = B * T
TILE = 3 * T
NT = 6
PADTOK = NT * TILE
H, DH, M = 12, 16, 100
HD = D // 2
HH = H // 2
S, F = 64, 768
GS = 4
NG = S // GS
RING = 4
BP = 32
EPS = 1e-5

C_ID, C_G, C_IND, C_MK, C_MV, NCST = 0, 128, 256, 384, 390, 393


def rows_of(i):
    return TILE if i < NT - 1 else NTOK - TILE * (NT - 1)


def imgs_of(i):
    return rows_of(i) // T


def vit_tower(nc, xT_d, wT_d, cst_d, tok_b, w_attn, b_attn, w_proj, b_proj, w_mem, b_mem, w_alpha, b_alpha,
              memT_d, slots, scale, w1, b1, w2, b2, norm_w, out):
    with ExitStack() as ctx:
        def sb(name, n):
            return ctx.enter_context(nc.sbuf_tensor(name, [128, n], F32))

        def sem(name):
            return ctx.enter_context(nc.semaphore(name))

        GW = GS * F + (GS // 2) * F + GS * (F // 128) * D
        ring = sb("ring", RING * GW)
        front = sb("front", 11648)
        h = sb("h", NT * D)[:, :].rearrange("p (i d) -> p i d", i=NT)
        cst = sb("cst", NCST)
        tokb = sb("tokb", D)
        normb = sb("normb", D)
        a1T = sb("a1T", 2 * NTOK)[:, :].rearrange("p (k t) -> p k t", k=2)
        C = sb("C", PADTOK)
        stats = sb("stats", NT * 8)[:, :].rearrange("p (i c) -> p i c", i=NT)
        small = sb("small", 300)

        def w1a(r):
            return ring[:, r * GW:r * GW + GS * F].rearrange("p (s n) -> p s n", s=GS)

        def w1b(r):
            o = r * GW + GS * F
            return ring[:, o:o + GS // 2 * F].rearrange("p (s n) -> p s n", s=GS // 2)

        def w2r(r):
            o = r * GW + GS * F + GS // 2 * F
            return ring[:, o:(r + 1) * GW].rearrange("p (s c n) -> p s c n", s=GS, c=F // 128)

        def late(o, n):
            o += (RING - 1) * GW
            return ring[:, o:o + n]

        xT = late(0, 3456).rearrange("p (c t) -> p c t", c=6)
        wT = late(3456, 1152)
        weff = late(4608, 1152).rearrange("p (c o) -> p c o", c=6)
        Vb = late(0, 3072).rearrange("p (b n) -> p b n", b=B)
        Kb = late(3072, 1728).rearrange("p (b k n) -> p b k n", b=4, k=2)
        P1 = late(4800, 1800).rearrange("p (u n) -> p u n", u=3)
        P1T = late(6600, 1296).rearrange("p (u h t) -> p u h t", u=2, h=HH)
        x3 = late(6600, 864).rearrange("p (u k n) -> p u k n", u=4, k=2)
        Ps = late(7896, 1296).rearrange("p (u n) -> p u n", u=3)

        def fr(o, n):
            return front[:, o:o + n]

        wA = fr(0, 1152).rearrange("p (k n) -> p k n", k=2)
        wM = fr(1152, 768).rearrange("p (k n) -> p k n", k=2)
        xlT = fr(1920, 1296).rearrange("p (k t) -> p k t", k=2)
        qT = fr(3216, 1216).rearrange("p (k t) -> p k t", k=2)
        kT = fr(4432, 1152).rearrange("p (k t) -> p k t", k=2)
        wAl = fr(5584, 768).rearrange("p (k n) -> p k n", k=4)
        wP = fr(6352, 384).rearrange("p (k n) -> p k n", k=2)
        memT = fr(6736, 200).rearrange("p (k n) -> p k n", k=2)
        PT = fr(6936, 1024).rearrange("p (u g n) -> p u g n", u=2, g=4)
        am = fr(7960, 384).rearrange("p (u n) -> p u n", u=2)
        aT = fr(8344, 1152).rearrange("p (k t) -> p k t", k=2)
        MKb = fr(9496, 1200).rearrange("p (k n) -> p k n", k=2)
        MVz = fr(10696, 384).rearrange("p (h n) -> p h n", h=H)
        th = fr(0, 1152).rearrange("p (k t) -> p k t", k=2)
        sm = fr(1152, 1152).rearrange("p (k t) -> p k t", k=2)
        df = fr(2304, 1152).rearrange("p (k t) -> p k t", k=2)
        fT = fr(3456, 1152).rearrange("p (k t) -> p k t", k=2)
        xn = fr(0, 1152).rearrange("p (i d) -> p i d", i=NT)
        tok = fr(1152, 1152).rearrange("p (i d) -> p i d", i=NT)
        sq = fr(2304, 1152).rearrange("p (i d) -> p i d", i=NT)
        tokT = fr(4608, 1296).rearrange("p (k t) -> p k t", k=2)
        Le = fr(6936, 384).rearrange("p (i s) -> p i s", i=NT)
        LTe = fr(7320, 648)
        Dm = fr(8960, 1152).rearrange("p (i b s) -> p i b s", i=NT, b=3)
        yA = fr(10112, 1024).rearrange("p (s b) -> p s b", s=S)
        yB = fr(11136, 512).rearrange("p (s b) -> p s b", s=S // 2)
        hg = fr(0, 1536).rearrange("p (u n) -> p u n", u=2)
        hT = fr(1536, 1536).rearrange("p (u c m) -> p u c m", u=2, c=6)
        b1g = fr(3072, 1536).rearrange("p (u n) -> p u n", u=2)
        ys = fr(4608, 512).rearrange("p (u w j b) -> p u w j b", u=2, w=2, j=GS)
        y2 = fr(5120, 384).rearrange("p (u n) -> p u n", u=2)
        Y = fr(5504, 3072).rearrange("p (b n) -> p b n", b=B)
        h1p = fr(8576, 1536).rearrange("p (i d) -> p i d", i=B // 2)

        xl = sb("xl", 2 * D)[:, :].rearrange("p (u d) -> p u d", u=2)
        bnst, epsc, b2s = sb("bnst", 6), sb("epsc", 1), sb("b2s", D)
        slr, squares = fr(11080, D), fr(11272, D)
        slT = fr(11464, 2 * S).rearrange("p (k s) -> p k s", k=2)

        ident = cst[:, C_ID:C_ID + 128]
        dct = cst[:, C_G:C_G + 128]
        ind4 = cst[0:GS, C_IND:C_IND + 128]
        mask_k = cst[0:HD, C_MK:C_MK + HH]
        mask_v = cst[0:TILE, C_MV:C_MV + 3]

        bank = [ctx.enter_context(nc.psum_tensor(f"bank{i}", [128, 512], F32)) for i in range(8)]

        ld_cst, ld_wT, ld_x, ld_mem, ld_attn, ld_rows, ld_late = (sem("ld_" + n) for n in (
            "cst", "wT", "x", "mem", "attn", "rows", "late"))
        ld_w1 = [sem(f"ld_w1_{r}") for r in range(RING)]
        ld_w2 = [sem(f"ld_w2_{r}") for r in range(RING)]
        ld_b1 = [sem(f"ld_b1_{u}") for u in range(2)]
        filled = sem("filled")
        dve = sem("dve_chain")
        act = sem("act_chain")
        pool = sem("pool_chain")
        names = ("weff_ps weff_sb h_ps h_sb var_sb std_sb xl_sb xlT_ps xlT_sb x3_sb qk_ps q_sb k_sb v_ps v_sb mk_ps mk_sb "
                 "mv_ps mv_sb slsq sl_std sl_sb slT_ps slT_sb kb_sb s1_ps p1_sub p1_exp p1_rec p1_norm p1T_ps p1T_sb "
                 "a1T_ps a1T_sb s_ps p_sub p_exp pT_ps pT_sb av_ps a_sb aT_ps aT_sb al_ps th_sb sumdif fT_sb pr_ps h1_sb "
                 "var2 std2 xl2 ms2 rstd2 xn_sb nn2 rn2 tok_sb tokT_ps tokT_sb L_ps L_sub L_exp L_nrm LT_ps LT_sub LT_exp "
                 "LT_nrm C_ps C_sb D_ps D_sb y_ps y_sb h1p_ld cb_ps h1b_sb "
                 "ys_sb g1_ps gelu_sb hT_ps hT_sb y2_ps y2_sb o_ps o_sb stored").split()
        sg = {n: sem(n) for n in names}
        y_ld = [sem(f"y_ld_{u}") for u in range(2)]

        block = ctx.enter_context(nc.Block())
        NB = B // 2
        NU = 2 * NT
        STEPS = NU + 3

        @block.sync
        def _(sp):
            sp.dma_start(cst[:, :], cst_d).then_inc(ld_cst, 16)
            sp.dma_start(wT, wT_d).then_inc(ld_wT, 16)
            sp.dma_start(xT, xT_d.rearrange("p (c t) -> p c t", c=6)).then_inc(ld_x, 16)

            def load_group(g, r):
                sp.dma_start(w1a(r), w1[bass.ds(g * GS, GS), 0:128, :].rearrange("s p n -> p s n")).then_inc(ld_w1[r], 16)
                v = w1[bass.ds(g * GS, GS), 128:D, :].rearrange("(q e) p n -> e p q n", e=2)
                for e in range(2):
                    sp.dma_start(w1b(r)[64 * e:64 * e + 64], v[e]).then_inc(ld_w1[r], 16)
                sp.dma_start(w2r(r), w2[bass.ds(g * GS, GS), :, :].rearrange("s (p c) n -> p s c n", c=6)).then_inc(ld_w2[r], 16)

            for r in range(RING):
                if r == RING - 1:
                    sp.wait_ge(sg["aT_sb"], NB)
                    sp.wait_ge(sg["a1T_sb"], NU)
                load_group(r, r)
            with sp.Fori(1, NG // RING) as i:
                for r in range(RING):
                    sp.wait_ge(sg["y2_ps"], (i - 1) * RING + r + 1)
                    load_group(i * RING + r, r)

            ov = out.rearrange("(i e) t d -> e t i d", e=2)
            for q in range(4):
                sp.wait_ge(sg["o_sb"], q + 1)
                for e in range(2):
                    sp.dma_start(ov[e][:, 2 * q:2 * q + 2, :], h1p[64 * e:64 * e + T, 2 * q:2 * q + 2, :]).then_inc(sg["stored"], 16)
            sp.wait_ge(sg["stored"], 8 * 16)

        @block.gpsimd
        def _(gp):
            ended = {}

            def alone(ins, ready=pool):
                ended[ready.name] = ended.get(ready.name, 0) + 1
                ins.then_inc(ready, 1)
                gp.wait_ge(ready, ended[ready.name])

            alone(gp.memset(memT[96:97, 1, :], 1.0), filled)
            alone(gp.memset(xlT[96:97, :, :], 1.0), filled)
            alone(gp.memset(aT[96:97, 1, :], 1.0), filled)
            alone(gp.memset(qT[:, :, NTOK:608], 0.0), filled)
            alone(gp.memset(MVz[:, :, :], 0.0), filled)
            alone(gp.memset(h[:, NT - 1, :], 0.0), filled)
            alone(gp.memset(epsc[:, :], EPS), filled)

            def k_blocks(i):
                gp.wait_ge(sg["k_sb"], 4)
                if i >= 2:
                    gp.wait_ge(sg["s_ps"], i - 1)
                for e in range(2):
                    b = 2 * i + e
                    for k in range(2):
                        alone(gp.tensor_tensor(
                            Kb[0:HD, b % 4, k, :].rearrange("p (h t) -> p h t", h=HH),
                            kT[0:HD, k, b * T:b * T + T].unsqueeze(1).broadcast_to([HD, HH, T]),
                            mask_k.unsqueeze(2).broadcast_to([HD, HH, T]), ALU.mult), sg["kb_sb"] if e == k == 1 else pool)

            gp.wait_ge(sg["xlT_sb"], NT)
            for b in range(B):
                if b >= 4 and b % 2 == 0:
                    gp.wait_ge(sg["v_ps"], b // 2 - 1)
                alone(gp.tensor_copy(x3[0:97, b % 4, :, :].rearrange("p k (r t) -> p k r t", r=3),
                               xlT[0:97, :, b * T:b * T + T].unsqueeze(2).broadcast_to([97, 2, 3, T])), sg["x3_sb"])
            gp.wait_ge(ld_cst, 16)
            k_blocks(0)
            for n in range(NU):
                if n + 1 < NB:
                    k_blocks(n + 1)
                i, hf = divmod(n, 2)
                r = rows_of(i)
                gp.wait_ge(sg["p1_rec"], n + 1)
                v = P1[0:r, n % 3, :].rearrange("p (h m) -> p h m", h=HH)
                alone(gp.tensor_tensor(v, v, small[0:r, 24 * (n % 3) + 12:24 * (n % 3) + 18].unsqueeze(2).broadcast_to([r, HH, M]),
                                       ALU.mult), sg["p1_norm"])

            gp.wait_ge(sg["aT_sb"], NB)
            gp.wait_ge(sg["a1T_sb"], NU)
            alone(gp.memset(fT[96:97, 1, :], 2.0), filled)
            alone(gp.memset(LTe[0:S, NTOK:PADTOK], 0.0), filled)
            for k in range(2):
                alone(gp.tensor_tensor(df[0:HD, k, :], aT[0:HD, k, :], a1T[0:HD, k, :], ALU.subtract), sg["sumdif"])
                alone(gp.tensor_tensor(sm[0:HD, k, :], aT[0:HD, k, :], a1T[0:HD, k, :], ALU.add), sg["sumdif"])

            gp.wait_ge(sg["h1b_sb"], NT)
            gp.wait_ge(sg["y_sb"], 3 * NT)
            for b in range(B):
                p = 36 * (b % 3)
                q = 64 * (b % 2)
                gp.dma_start(h1p[q:q + T, b // 2, :], h[p:p + T, b // 3, :]).then_inc(sg["h1p_ld"], 16)
            for g in range(NG):
                gp.wait_ge(sg["y2_sb"], g + 1)
                for j in range(GS):
                    s = g * GS + j
                    gp.dma_start(Y[s:s + 1, :, :], y2[32 * j:32 * j + B, g % 2, :]).then_inc(y_ld[g % 2], 16)

        @block.scalar
        def _(sc):
            half = "(k p) n -> p k n"
            sc.dma_start(memT[0:HD], memT_d.rearrange(half, k=2)).then_inc(ld_mem, 16)
            sc.dma_start(wM[0:HD], w_mem.rearrange(half, k=2)).then_inc(ld_mem, 16)
            sc.dma_start(wM[96:97, 1, :], b_mem.unsqueeze(0)).then_inc(ld_mem, 16)
            sc.dma_start(tokb[:, :], tok_b.unsqueeze(0).broadcast_to([128, D])).then_inc(ld_rows, 16)
            sc.dma_start(normb[:, :], norm_w.unsqueeze(0).broadcast_to([128, D])).then_inc(ld_rows, 16)
            sc.dma_start(slr[0:S, :], slots).then_inc(ld_rows, 16)
            sc.dma_start(small[0:S, 299:300], scale.unsqueeze(1)).then_inc(ld_rows, 16)
            sc.dma_start(wA[0:HD], w_attn.rearrange(half, k=2)).then_inc(ld_attn, 16)
            sc.dma_start(wA[96:97, 1, :], b_attn.unsqueeze(0)).then_inc(ld_attn, 16)
            sc.dma_start(wAl[0:HD], w_alpha.rearrange("(k p) n -> p k n", k=4)).then_inc(ld_late, 16)
            sc.dma_start(wAl[96:97, 1, :], b_alpha.unsqueeze(0)).then_inc(ld_late, 16)
            sc.dma_start(wP[0:HD], w_proj.rearrange(half, k=2)).then_inc(ld_late, 16)
            sc.dma_start(wP[96:97, 1, :], b_proj.unsqueeze(0)).then_inc(ld_late, 16)
            sc.dma_start(b2s[0:S, :], b2).then_inc(ld_late, 16)

            def xlT_copy(i):
                sc.wait_ge(sg["xlT_ps"], i + 1)
                n = rows_of(i)
                sc.activation(xlT[0:HD, :, i * TILE:i * TILE + n],
                              bank[1 + i % 2][0:HD, 0:2 * TILE].rearrange("p (k t) -> p k t", k=2)[:, :, 0:n], ACT.Copy)\
                    .then_inc(sg["xlT_sb"], 1)

            sc.wait_ge(ld_rows, 64)
            sc.activation(squares[0:S, :], slr[0:S, :], ACT.Square, accum_out=small[0:S, 290:291]).then_inc(act, 1)
            sc.wait_ge(act, 1)
            sc.activation(small[0:S, 291:292], small[0:S, 290:291], ACT.Sqrt).then_inc(sg["sl_std"], 1)
            for i in range(NT):
                sc.wait_ge(sg["var_sb"], i + 1)
                sc.activation(stats[0:TILE, i, 3:4], stats[0:TILE, i, 2:3], ACT.Sqrt).then_inc(sg["std_sb"], 1)
                if i >= 1:
                    xlT_copy(i - 1)
            xlT_copy(NT - 1)
            for u in range(4):
                m, n = divmod(u, 2)
                sc.wait_ge(sg["qk_ps"], u + 1)
                sc.activation(qT[0:HD, m, n * 288:n * 288 + 288], bank[3 + u % 4][0:HD, 0:288], ACT.Copy).then_inc(sg["q_sb"], 1)

            for n in range(STEPS):
                if n < NU:
                    r = rows_of(n // 2)
                    sc.wait_ge(sg["p1_sub"], n + 1)
                    sc.activation(P1[0:r, n % 3, :], P1[0:r, n % 3, :], ACT.Exp).then_inc(sg["p1_exp"], 1)
                if n < NB:
                    sc.wait_ge(sg["p_sub"], n + 1)
                    sc.activation(Ps[:, n % 3, :], Ps[:, n % 3, :], ACT.Exp).then_inc(sg["p_exp"], 1)
                if 0 <= n - 1 < NU:
                    u = n - 1
                    r = rows_of(u // 2)
                    sc.wait_ge(sg["p1T_ps"], u + 1)
                    if u >= 2:
                        sc.wait_ge(sg["a1T_ps"], u - 1)
                    for q in range(2):
                        ins = sc.activation(P1T[0:M, u % 2, 3 * q:3 * q + 3, 0:r],
                                            bank[4 + q][0:M, 0:3 * TILE].rearrange("p (h t) -> p h t", h=3)[:, :, 0:r], ACT.Copy)
                    ins.then_inc(sg["p1T_sb"], 1)
                if 0 <= n - 1 < NB:
                    u = n - 1
                    sc.wait_ge(sg["pT_ps"], u + 1)
                    if u >= 2:
                        sc.wait_ge(sg["av_ps"], u - 1)
                    sc.activation(PT[0:TILE, u % 2, :, :], bank[1][0:TILE, :].rearrange("p (g m) -> p g m", g=4), ACT.Copy)\
                        .then_inc(sg["pT_sb"], 1)
                if 0 <= n - 2 < NU:
                    u = n - 2
                    i, k = divmod(u, 2)
                    r = rows_of(i)
                    sc.wait_ge(sg["a1T_ps"], u + 1)
                    sc.activation(a1T[0:HD, k, i * TILE:i * TILE + r], bank[6][0:HD, 0:r], ACT.Copy).then_inc(sg["a1T_sb"], 1)
                if 0 <= n - 3 < NB:
                    u = n - 3
                    sc.wait_ge(sg["aT_ps"], u + 1)
                    sc.activation(aT[0:HD, :, 2 * T * u:2 * T * (u + 1)].rearrange("p k (e t) -> p k e t", e=2),
                                  bank[6][0:HD, 256:512].rearrange("p (k e t) -> p k e t", k=2, e=2)[:, :, :, 0:T],
                                  ACT.Copy).then_inc(sg["aT_sb"], 1)

            for u in range(4):
                m, n = divmod(u, 2)
                sc.wait_ge(sg["al_ps"], u + 1)
                sc.activation(th[0:HD, m, n * 288:n * 288 + 288], bank[u][0:HD, 0:288], ACT.Tanh, scale=0.5).then_inc(sg["th_sb"], 1)

            for i in range(NT):
                sc.wait_ge(sg["var2"], i + 1)
                sc.activation(stats[0:TILE, i, 3:4], stats[0:TILE, i, 2:3], ACT.Sqrt).then_inc(sg["std2"], 1)
            for i in range(NT):
                sc.wait_ge(sg["xl2"], i + 1)
                sc.activation(sq[0:TILE, i, :], xn[0:TILE, i, :], ACT.Square, accum_out=small[0:TILE, 100 + i:101 + i]).then_inc(act, 1)
            sc.wait_ge(act, 1 + NT)
            sc.wait_ge(filled, 7)
            sc.activation(small[0:TILE, 110:116], small[0:TILE, 100:106], ACT.Sqrt, scale=1.0 / D, bias=epsc[0:TILE, 0:1]).then_inc(sg["ms2"], 1)
            for i in range(NT):
                sc.wait_ge(sg["xn_sb"], i + 1)
                sc.activation(sq[0:TILE, i, :], xn[0:TILE, i, :], ACT.Square, accum_out=small[0:TILE, 120 + i:121 + i]).then_inc(act, 1)
            sc.wait_ge(act, 1 + 2 * NT)
            sc.activation(small[0:TILE, 130:136], small[0:TILE, 120:126], ACT.Sqrt).then_inc(sg["nn2"], 1)
            for i in range(NT):
                sc.wait_ge(sg["tokT_ps"], i + 1)
                sc.activation(tokT[0:HD, :, i * TILE:(i + 1) * TILE],
                              bank[4 + i % 2][0:HD, 0:2 * TILE].rearrange("p (k t) -> p k t", k=2), ACT.Copy).then_inc(sg["tokT_sb"], 1)
            sc.wait_ge(sg["LT_sub"], 1)
            sc.activation(LTe[0:S, 0:NTOK], LTe[0:S, 0:NTOK], ACT.Exp).then_inc(sg["LT_exp"], 1)
            sc.wait_ge(sg["L_sub"], 1)
            sc.activation(Le[0:TILE], Le[0:TILE], ACT.Exp).then_inc(sg["L_exp"], 1)

            def gelu(n, u):
                for q in range(2):
                    sc.wait_ge(sg["g1_ps"], n * 2 + q + 1)
                    sc.activation(hg[:, u, q * 384:q * 384 + 384], bank[q][:, 0:384], ACT.Gelu).then_inc(sg["gelu_sb"], 1)

            def biases(g, u):
                sc.dma_start(b1g[0:GS, u, :], b1[bass.ds(g * GS, GS), :]).then_inc(ld_b1[u], 16)

            sc.wait_ge(sg["y_sb"], 3 * NT)
            biases(0, 0)
            biases(1, 1)
            with sc.Fori(0, NG // RING - 1) as i:
                for r in range(RING):
                    gelu(i * RING + r, r % 2)
                    biases(i * RING + (r + 2), r % 2)
            for r in range(RING):
                gelu((NG // RING - 1) * RING + r, r % 2)
                if r < 2:
                    biases(NG - RING + r + 2, r % 2)

        @block.vector
        def _(ve):
            chain = [0]

            def link(ins):
                chain[0] += 1
                ins.then_inc(dve, 1)
                ve.wait_ge(dve, chain[0])

            ve.wait_ge(ld_cst, 16)
            ve.wait_ge(sg["mk_ps"], 1)
            for k in range(2):
                ins = ve.tensor_tensor(MKb[0:HD, k, :].rearrange("p (h m) -> p h m", h=HH),
                                       bank[5][0:HD, k * M:k * M + M].unsqueeze(1).broadcast_to([HD, HH, M]),
                                       mask_k.unsqueeze(2).broadcast_to([HD, HH, M]), ALU.mult)
            ins.then_inc(sg["mk_sb"], 1)
            ve.wait_ge(sg["mv_ps"], 1)
            ve.wait_ge(filled, 5)
            for e in range(2):
                ins = ve.tensor_copy(MVz[0:M, e::2, DH * e:DH * e + DH],
                                     bank[6][0:M, 0:D].rearrange("p (h e c) -> p h e c", e=2, c=DH)[:, :, e, :])
            ins.then_inc(sg["mv_sb"], 1)
            for q in range(3):
                ve.wait_ge(sg["weff_ps"], q + 1)
                ve.tensor_copy(weff[:, 2 * q:2 * q + 2, :], bank[q][:, 0:384].rearrange("p (c o) -> p c o", c=2))\
                    .then_inc(sg["weff_sb"], 1)
            ve.wait_ge(sg["sl_std"], 1)
            link(ve.tensor_scalar(small[0:S, 292:293], small[0:S, 291:292], EPS, None, ALU.max))
            link(ve.reciprocal(small[0:S, 293:294], small[0:S, 292:293]))
            ve.tensor_scalar(slr[0:S, :], slr[0:S, :], small[0:S, 293:294], small[0:S, 299:300], ALU.mult, ALU.mult)\
                .then_inc(sg["sl_sb"], 1)

            ve.wait_ge(sg["slT_ps"], 1)
            ve.tensor_copy(slT[0:HD, :, :], bank[7][0:HD, 0:2 * S].rearrange("p (k s) -> p k s", k=2)).then_inc(sg["slT_sb"], 1)

            def moments(i):
                link(ve.bn_stats(bnst[0:TILE, :], h[0:TILE, i, :]))
                link(ve.bn_aggr(stats[0:TILE, i, 0:2], bnst[0:TILE, :]))
                return ve.tensor_scalar(stats[0:TILE, i, 2:3], stats[0:TILE, i, 1:2], EPS, None, ALU.add)

            def normalise(dst, i):
                link(ve.reciprocal(stats[0:TILE, i, 4:5], stats[0:TILE, i, 3:4]))
                return ve.tensor_scalar(dst, h[0:TILE, i, :], stats[0:TILE, i, 0:1], stats[0:TILE, i, 4:5],
                                        ALU.subtract, ALU.mult)

            ve.wait_ge(filled, 6)
            for i in range(NT + 1):
                if i < NT:
                    r = rows_of(i)
                    ve.wait_ge(sg["h_ps"], i + 1)
                    link(ve.tensor_tensor(h[0:r, i, :], bank[(3 + i) % 8][0:r, 0:D], tokb[0:r, :], ALU.add))
                    moments(i).then_inc(sg["var_sb"], 1)
                if i >= 1:
                    ve.wait_ge(sg["std_sb"], i)
                    if i >= 3:
                        ve.wait_ge(sg["xlT_ps"], i - 2)
                    normalise(xl[0:TILE, (i - 1) % 2, :], i - 1).then_inc(sg["xl_sb"], 1)

            for u in range(4, 8):
                m, n = divmod(u - 4, 2)
                ve.wait_ge(sg["qk_ps"], u + 1)
                ve.tensor_copy(kT[0:HD, m, n * 288:n * 288 + 288], bank[3 + u % 4][0:HD, 0:288]).then_inc(sg["k_sb"], 1)
            for p in range(NB):
                ve.wait_ge(sg["v_ps"], p + 1)
                for e in range(2):
                    ins = ve.tensor_tensor(
                        Vb[0:TILE, 2 * p + e, :].rearrange("p (g r c) -> p g r c", g=4, r=3),
                        bank[(7, 0)[p % 2]][0:TILE, e * 256:e * 256 + D].rearrange("p (g r c) -> p g r c", g=4, r=3),
                        mask_v.unsqueeze(1).unsqueeze(3).broadcast_to([TILE, 4, 3, DH]), ALU.mult)
                ins.then_inc(sg["v_sb"], 1)

            for n in range(STEPS):
                if n < NU:
                    r = rows_of(n // 2)
                    s1 = [bank[2 + q][0:r, 0:300].rearrange("p (h m) -> p h m", h=3) for q in range(2)]
                    mx = small[0:r, 24 * (n % 3):24 * (n % 3) + 6]
                    ve.wait_ge(sg["s1_ps"], n + 1)
                    if n >= 3:
                        ve.wait_ge(sg["p1T_ps"], n - 2)
                    ve.tensor_reduce(mx[:, 0:3], s1[0], AX.X, ALU.max)
                    link(ve.tensor_reduce(mx[:, 3:6], s1[1], AX.X, ALU.max))
                    for q in range(2):
                        ins = ve.tensor_tensor(P1[0:r, n % 3, q * 300:q * 300 + 300].rearrange("p (h m) -> p h m", h=3), s1[q],
                                               mx[:, 3 * q:3 * q + 3].unsqueeze(2).broadcast_to([r, 3, M]), ALU.subtract)
                    ins.then_inc(sg["p1_sub"], 1)
                if n < NB:
                    ve.wait_ge(sg["s_ps"], n + 1)
                    if n >= 3:
                        ve.wait_ge(sg["pT_ps"], n - 2)
                    sv = bank[0][:, 0:432].rearrange("p (h t) -> p h t", h=H)
                    mx = small[:, 140 + 36 * (n % 3):152 + 36 * (n % 3)]
                    link(ve.tensor_reduce(mx, sv, AX.X, ALU.max))
                    ve.tensor_tensor(Ps[:, n % 3, :].rearrange("p (h t) -> p h t", h=H), sv,
                                     mx.unsqueeze(2).broadcast_to([128, H, T]), ALU.subtract).then_inc(sg["p_sub"], 1)
                if n < NU:
                    r = rows_of(n // 2)
                    o = 24 * (n % 3)
                    ve.wait_ge(sg["p1_exp"], n + 1)
                    link(ve.tensor_reduce(small[0:r, o + 6:o + 12], P1[0:r, n % 3, :].rearrange("p (h m) -> p h m", h=HH), AX.X, ALU.add))
                    ve.reciprocal(small[0:r, o + 12:o + 18], small[0:r, o + 6:o + 12]).then_inc(sg["p1_rec"], 1)
                if n < NB:
                    o = 140 + 36 * (n % 3)
                    ve.wait_ge(sg["p_exp"], n + 1)
                    link(ve.tensor_reduce(small[:, o + 12:o + 24], Ps[:, n % 3, :].rearrange("p (h t) -> p h t", h=H), AX.X, ALU.add))
                    link(ve.reciprocal(small[:, o + 24:o + 36], small[:, o + 12:o + 24]))
                if 0 <= n - 2 < NB:
                    u = n - 2
                    o = 140 + 36 * (u % 3) + 24
                    ve.wait_ge(sg["av_ps"], u + 1)
                    if u >= 2:
                        ve.wait_ge(sg["aT_ps"], u - 1)
                    ve.tensor_tensor(am[:, u % 2, :].rearrange("p (h c) -> p h c", h=H),
                                     bank[7][:, 0:D].rearrange("p (h c) -> p h c", h=H),
                                     small[:, o:o + H].unsqueeze(2).broadcast_to([128, H, DH]), ALU.mult).then_inc(sg["a_sb"], 1)

            ve.wait_ge(sg["sumdif"], 4)
            for k in range(2):
                ve.wait_ge(sg["th_sb"], 2 * k + 2)
                link(ve.tensor_tensor(df[0:HD, k, :], df[0:HD, k, :], th[0:HD, k, :], ALU.mult))
                ve.tensor_tensor(fT[0:HD, k, :], df[0:HD, k, :], sm[0:HD, k, :], ALU.add).then_inc(sg["fT_sb"], 1)

            for i in range(NT):
                r = rows_of(i)
                ve.wait_ge(sg["pr_ps"], i + 1)
                link(ve.scalar_tensor_tensor(out=h[0:r, i, :], in0=bank[4 + i % 4][0:r, 0:D], scalar=0.5, in1=h[0:r, i, :],
                                             op0=ALU.mult, op1=ALU.add))
                moments(i).then_inc(sg["var2"], 1)
            for i in range(NT):
                ve.wait_ge(sg["std2"], i + 1)
                normalise(xn[0:TILE, i, :], i).then_inc(sg["xl2"], 1)
            ve.wait_ge(sg["ms2"], 1)
            link(ve.reciprocal(small[0:TILE, 110:116], small[0:TILE, 110:116]))
            for i in range(NT):
                ve.scalar_tensor_tensor(out=xn[0:TILE, i, :], in0=xn[0:TILE, i, :], scalar=small[0:TILE, 110 + i:111 + i],
                                        in1=normb[0:TILE, :], op0=ALU.mult, op1=ALU.mult).then_inc(sg["xn_sb"], 1)
            ve.wait_ge(sg["nn2"], 1)
            link(ve.tensor_scalar(small[0:TILE, 130:136], small[0:TILE, 130:136], EPS, None, ALU.max))
            link(ve.reciprocal(small[0:TILE, 130:136], small[0:TILE, 130:136]))
            for i in range(NT):
                ve.tensor_scalar(tok[0:TILE, i, :], xn[0:TILE, i, :], small[0:TILE, 130 + i:131 + i], None, ALU.mult)\
                    .then_inc(sg["tok_sb"], 1)

            ve.wait_ge(sg["LT_ps"], 2)
            lt = [bank[q][0:S, 0:288].rearrange("p (b t) -> p b t", b=8) for q in range(2)]
            for q in range(2):
                ins = ve.tensor_reduce(small[0:S, 8 * q:8 * q + 8], lt[q], AX.X, ALU.max)
            link(ins)
            for q in range(2):
                ins = ve.tensor_tensor(LTe[0:S, 288 * q:288 * q + 288].rearrange("p (b t) -> p b t", b=8), lt[q],
                                       small[0:S, 8 * q:8 * q + 8].unsqueeze(2).broadcast_to([S, 8, T]), ALU.subtract)
            ins.then_inc(sg["LT_sub"], 1)
            ve.wait_ge(sg["L_ps"], 1)
            lv = bank[2][0:TILE, 0:384].rearrange("p (i s) -> p i s", i=NT)
            link(ve.tensor_reduce(small[0:TILE, 20:26], lv, AX.X, ALU.max))
            ve.tensor_tensor(Le[0:TILE], lv, small[0:TILE, 20:26].unsqueeze(2).broadcast_to([TILE, NT, S]), ALU.subtract)\
                .then_inc(sg["L_sub"], 1)
            ve.wait_ge(sg["LT_exp"], 1)
            le = LTe[0:S, 0:NTOK].rearrange("p (b t) -> p b t", b=B)
            link(ve.tensor_reduce(small[0:S, 30:46], le, AX.X, ALU.add))
            link(ve.reciprocal(small[0:S, 50:66], small[0:S, 30:46]))
            ve.tensor_tensor(le, le, small[0:S, 50:66].unsqueeze(2).broadcast_to([S, B, T]), ALU.mult).then_inc(sg["LT_nrm"], 1)
            ve.wait_ge(sg["L_exp"], 1)
            link(ve.tensor_reduce(small[0:TILE, 70:76], Le[0:TILE], AX.X, ALU.add))
            link(ve.reciprocal(small[0:TILE, 80:86], small[0:TILE, 70:76]))
            ve.tensor_tensor(Le[0:TILE], Le[0:TILE], small[0:TILE, 80:86].unsqueeze(2).broadcast_to([TILE, NT, S]), ALU.mult)\
                .then_inc(sg["L_nrm"], 1)
            ve.wait_ge(sg["D_ps"], 1)
            dp = bank[3][0:TILE, 0:384].rearrange("p (i s) -> p i s", i=NT)
            for b in range(3):
                ins = ve.tensor_scalar(Dm[0:TILE, :, b, :], dp, mask_v[:, b:b + 1], None, ALU.mult)
            ins.then_inc(sg["D_sb"], 1)
            for i in range(NT):
                m = imgs_of(i)
                ve.wait_ge(sg["y_ps"], i + 1)
                bk = bank[4 + i % 2]
                ve.tensor_copy(yA[:, :, 3 * i:3 * i + m].rearrange("p s b -> p b s"),
                               bk[:, 0:m * S].rearrange("p (b s) -> p b s", b=m)).then_inc(sg["y_sb"], 1)
                for e in range(2):
                    p = slice(64 * e, 64 * e + 64)
                    ve.tensor_copy(yB[p, :, 3 * i:3 * i + m].rearrange("p s b -> p b s"),
                                   bk[p, 256:256 + m * S // 2].rearrange("p (b s) -> p b s", b=m)).then_inc(sg["y_sb"], 1)
            for q in range(2):
                ve.wait_ge(sg["C_ps"], q + 1)
                ve.tensor_copy(C[0:S, 324 * q:324 * q + 324], bank[6 + q][0:S, 0:324]).then_inc(sg["C_sb"], 1)
            for i in range(NT):
                r = rows_of(i)
                ve.wait_ge(sg["cb_ps"], i + 1)
                ve.tensor_tensor(h[0:r, i, :], bank[2 + i % 2][0:r, 0:D], h[0:r, i, :], ALU.add).then_inc(sg["h1b_sb"], 1)

            ve.wait_ge(sg["y_ps"], NT)
            link(ve.memset(ys[:, :, :, :, :], 0.0))

            def stationary(g, u):
                ve.tensor_copy(ys[:, u, 0, :, 0:B], yA[:, bass.ds(g * GS, GS), :])
                for e in range(2):
                    p = slice(64 * e, 64 * e + 64)
                    ins = ve.tensor_copy(ys[p, u, 1, e::2, 0:B], yB[p, bass.ds(g * (GS // 2), GS // 2), :])
                ins.then_inc(sg["ys_sb"], 1)

            def answers(n, u):
                for q in range(2):
                    ve.wait_ge(sg["hT_ps"], 2 * n + q + 1)
                    ve.tensor_copy(hT[:, u, 3 * q:3 * q + 3, :], bank[2 + q][:, 0:384].rearrange("p (c m) -> p c m", c=3))\
                        .then_inc(sg["hT_sb"], 1)

            def gather(n, u):
                ve.wait_ge(sg["y2_ps"], n + 1)
                ve.tensor_copy(y2[:, u, :], bank[4 + u][:, 0:D]).then_inc(sg["y2_sb"], 1)

            stationary(0, 0)
            stationary(1, 1)
            for r in range(2):
                answers(r, r)
                gather(r, r)
                stationary(r + 2, r % 2)
            with ve.Fori(0, (NG - 4) // 4) as i:
                for r in range(4):
                    n = i * 4 + (r + 2)
                    answers(n, r % 2)
                    ve.wait_ge(y_ld[r % 2], 128 * i + 64 * ((r + 2) // 2))
                    gather(n, r % 2)
                    stationary(n + 2, r % 2)
            for n in range(NG - 2, NG):
                answers(n, n % 2)
                ve.wait_ge(y_ld[n % 2], 64 * (n // 2))
                gather(n, n % 2)

            ve.wait_ge(sg["h1p_ld"], 16 * B)
            for q in range(4):
                ve.wait_ge(sg["o_ps"], q + 1)
                for e in range(2):
                    p = slice(64 * e, 64 * e + T)
                    v = h1p[p, 2 * q:2 * q + 2, :]
                    ins = ve.tensor_tensor(v, v, bank[q][p, 0:384].rearrange("p (i d) -> p i d", i=2), ALU.add)
                ins.then_inc(sg["o_sb"], 1)

        @block.tensor
        def _(pe):
            def kr(k):
                return HD + k

            pe.wait_ge(ld_mem, 48)
            pe.wait_ge(filled, 1)
            for m in range(2):
                for k in range(2):
                    mm = pe.matmul(bank[5][0:HD, m * M:m * M + M], wM[0:kr(k), k, m * HD:m * HD + HD], memT[0:kr(k), k, :],
                                   start=(k == 0), stop=(k == 1))
            mm.then_inc(sg["mk_ps"], 1)
            for k in range(2):
                mm = pe.matmul(bank[6][0:M, 0:D], memT[0:kr(k), k, :], wM[0:kr(k), k, D:2 * D], start=(k == 0), stop=(k == 1))
            mm.then_inc(sg["mv_ps"], 1)
            pe.wait_ge(ld_cst, 16)
            pe.wait_ge(ld_wT, 16)
            for q in range(3):
                pe.matmul(bank[q][:, 0:384], dct, wT[:, q * 384:q * 384 + 384], start=True, stop=True).then_inc(sg["weff_ps"], 1)
            pe.wait_ge(sg["sl_sb"], 1)
            for k in range(2):
                mm = pe.transpose(bank[7][0:HD, k * S:k * S + S], slr[0:S, k * HD:k * HD + HD], ident[0:S, 0:S])
            mm.then_inc(sg["slT_ps"], 1)
            pe.wait_ge(ld_x, 16)
            pe.wait_ge(sg["weff_sb"], 3)
            pe.wait_ge(sg["mk_sb"], 1)
            pe.wait_ge(sg["mv_sb"], 1)
            pe.wait_ge(sg["slT_sb"], 1)

            def xl_transpose(i):
                pe.wait_ge(sg["xl_sb"], i + 1)
                if i >= 2:
                    pe.wait_ge(sg["xlT_sb"], i - 1)
                for k in range(2):
                    mm = pe.transpose(bank[1 + i % 2][0:HD, k * TILE:k * TILE + TILE], xl[0:TILE, i % 2, k * HD:k * HD + HD],
                                      ident[0:TILE, 0:TILE])
                mm.then_inc(sg["xlT_ps"], 1)

            for i in range(NT):
                r = rows_of(i)
                for c in range(6):
                    mm = pe.matmul(bank[(3 + i) % 8][0:r, 0:D], xT[:, c, i * TILE:i * TILE + r], weff[:, c, :],
                                   start=(c == 0), stop=(c == 5))
                mm.then_inc(sg["h_ps"], 1)
                if i >= 2:
                    xl_transpose(i - 2)
            xl_transpose(NT - 2)
            xl_transpose(NT - 1)
            pe.wait_ge(ld_attn, 32)
            pe.wait_ge(sg["xlT_sb"], NT)
            pe.wait_ge(filled, 4)
            pe.wait_ge(sg["var_sb"], NT)
            for u in range(8):
                m, n = divmod(u, 2)
                if u == 4:
                    pe.wait_ge(sg["q_sb"], 1)
                if u >= 4:
                    pe.wait_ge(sg["q_sb"], u - 3)
                for k in range(2):
                    mm = pe.matmul(bank[3 + u % 4][0:HD, 0:288], wA[0:kr(k), k, m * HD:m * HD + HD],
                                   xlT[0:kr(k), k, n * 288:n * 288 + 288], start=(k == 0), stop=(k == 1))
                mm.then_inc(sg["qk_ps"], 1)
            for p in range(NB):
                if p >= 2:
                    pe.wait_ge(sg["v_sb"], p - 1)
                pe.wait_ge(sg["x3_sb"], 2 * p + 2)
                for e in range(2):
                    b = 2 * p + e
                    for k in range(2):
                        mm = pe.matmul(bank[(7, 0)[p % 2]][0:TILE, e * 256:e * 256 + D],
                                       x3[0:kr(k), b % 4, k, :],
                                       wA[0:kr(k), k, 2 * D:3 * D], start=(k == 0), stop=(k == 1))
                mm.then_inc(sg["v_ps"], 1)

            pe.wait_ge(sg["q_sb"], 4)
            pe.wait_ge(sg["k_sb"], 4)
            pe.wait_ge(sg["v_sb"], NB)
            for n in range(STEPS):
                if n < NU:
                    i, k = divmod(n, 2)
                    r = rows_of(i)
                    if n >= 1:
                        pe.wait_ge(sg["p1_sub"], n)
                    for q in range(2):
                        mm = pe.matmul(bank[2 + q][0:r, 0:300], qT[0:HD, k, i * TILE:i * TILE + r],
                                       MKb[0:HD, k, 300 * q:300 * q + 300], start=True, stop=True)
                    mm.then_inc(sg["s1_ps"], 1)
                if n < NB:
                    pe.wait_ge(sg["kb_sb"], n + 1)
                    if n >= 1:
                        pe.wait_ge(sg["p_sub"], n)
                    for k in range(2):
                        for e in range(2):
                            b = 2 * n + e
                            mm = pe.matmul(bank[0][64 * e:64 * e + 64, 216 * k:216 * k + 216], qT[0:HD, k, b * T:b * T + 64],
                                           Kb[0:HD, b % 4, k, :], start=True, stop=True)
                    mm.then_inc(sg["s_ps"], 1)
                if 0 <= n - 1 < NU:
                    u = n - 1
                    r = rows_of(u // 2)
                    pe.wait_ge(sg["p1_norm"], u + 1)
                    if u >= 1:
                        pe.wait_ge(sg["p1T_sb"], u)
                    for x in range(HH):
                        mm = pe.transpose(bank[4 + x // 3][0:M, (x % 3) * TILE:(x % 3) * TILE + r],
                                          P1[0:r, u % 3, x * M:x * M + M], ident[0:r, 0:r])
                    mm.then_inc(sg["p1T_ps"], 1)
                if 0 <= n - 1 < NB:
                    u = n - 1
                    pe.wait_ge(sg["p_exp"], u + 1)
                    if u >= 1:
                        pe.wait_ge(sg["pT_sb"], u)
                    for g in range(4):
                        mm = pe.transpose(bank[1][0:TILE, g * 128:g * 128 + 128], Ps[:, u % 3, g * TILE:g * TILE + TILE], ident)
                    mm.then_inc(sg["pT_ps"], 1)
                if 0 <= n - 2 < NU:
                    u = n - 2
                    i, k = divmod(u, 2)
                    r = rows_of(i)
                    pe.wait_ge(sg["p1T_sb"], u + 1)
                    if u >= 1:
                        pe.wait_ge(sg["a1T_sb"], u)
                    if u >= 2:
                        pe.wait_ge(sg["aT_sb"], min(u - 1, NB))
                    for par in range(2):
                        for c in range(3):
                            x = 2 * c + par
                            mm = pe.matmul(bank[6][32 * c:32 * c + 32, 0:r], MVz[0:M, k * HH + x, :], P1T[0:M, u % 2, x, 0:r],
                                           start=(par == 0), stop=(par == 1))
                    mm.then_inc(sg["a1T_ps"], 1)
                if 0 <= n - 2 < NB:
                    u = n - 2
                    pe.wait_ge(sg["pT_sb"], u + 1)
                    if u >= 1:
                        pe.wait_ge(sg["a_sb"], u)
                    for g in range(4):
                        for e in range(2):
                            mm = pe.matmul(bank[7][64 * e:64 * e + 64, g * 48:g * 48 + 48], PT[0:TILE, u % 2, g, 64 * e:64 * e + 64],
                                           Vb[0:TILE, 2 * u + e, g * 48:g * 48 + 48], start=True, stop=True)
                    mm.then_inc(sg["av_ps"], 1)
                if 0 <= n - 3 < NB:
                    u = n - 3
                    pe.wait_ge(sg["a_sb"], u + 1)
                    pe.wait_ge(sg["a1T_sb"], min(n - 1, NU))
                    for k in range(2):
                        mm = pe.transpose(bank[6][0:HD, 256 + 128 * k:256 + 128 * k + 128], am[:, u % 2, k * HD:k * HD + HD], ident)
                    mm.then_inc(sg["aT_ps"], 1)

            pe.wait_ge(ld_late, 80)
            pe.wait_ge(sg["aT_sb"], NB)
            pe.wait_ge(sg["a1T_sb"], NU)
            for u in range(4):
                m, n = divmod(u, 2)
                for k in range(4):
                    src = (aT, a1T)[k // 2]
                    rows = HD + (k == 1)
                    mm = pe.matmul(bank[u][0:HD, 0:288], wAl[0:rows, k, m * HD:m * HD + HD], src[0:rows, k % 2, n * 288:n * 288 + 288],
                                   start=(k == 0), stop=(k == 3))
                mm.then_inc(sg["al_ps"], 1)
            pe.wait_ge(sg["fT_sb"], 2)
            pe.wait_ge(filled, 8)
            for i in range(NT):
                r = rows_of(i)
                if i >= 4:
                    pe.wait_ge(sg["var2"], i - 3)
                for k in range(2):
                    mm = pe.matmul(bank[4 + i % 4][0:r, 0:D], fT[0:kr(k), k, i * TILE:i * TILE + r], wP[0:kr(k), k, :],
                                   start=(k == 0), stop=(k == 1))
                mm.then_inc(sg["pr_ps"], 1)
            pe.wait_ge(sg["var2"], NT)
            for i in range(NT):
                pe.wait_ge(sg["tok_sb"], i + 1)
                if i >= 2:
                    pe.wait_ge(sg["tokT_sb"], i - 1)
                for k in range(2):
                    mm = pe.transpose(bank[4 + i % 2][0:HD, k * TILE:k * TILE + TILE], tok[0:TILE, i, k * HD:k * HD + HD],
                                      ident[0:TILE, 0:TILE])
                mm.then_inc(sg["tokT_ps"], 1)
            pe.wait_ge(sg["tokT_sb"], NT)
            pe.wait_ge(sg["th_sb"], 4)
            for n in range(2):
                for k in range(2):
                    mm = pe.matmul(bank[n][0:S, 0:288], slT[0:HD, k, :], tokT[0:HD, k, n * 288:n * 288 + 288],
                                   start=(k == 0), stop=(k == 1))
                mm.then_inc(sg["LT_ps"], 1)
            for i in range(NT):
                for k in range(2):
                    mm = pe.matmul(bank[2][0:TILE, i * S:i * S + S], tokT[0:HD, k, i * TILE:i * TILE + TILE], slT[0:HD, k, :],
                                   start=(k == 0), stop=(k == 1))
            mm.then_inc(sg["L_ps"], 1)
            pe.wait_ge(sg["LT_nrm"], 1)
            pe.wait_ge(filled, 9)
            for i in range(NT):
                mm = pe.transpose(bank[3][0:TILE, i * S:i * S + S], LTe[0:S, i * TILE:i * TILE + TILE], ident[0:S, 0:S])
            mm.then_inc(sg["D_ps"], 1)
            pe.wait_ge(sg["D_sb"], 1)
            for i in range(NT):
                m = imgs_of(i)
                if i >= 2:
                    pe.wait_ge(sg["y_sb"], 3 * (i - 1))
                bk = bank[4 + i % 2]
                pe.matmul(bk[:, 0:m * S], xn[0:TILE, i, 0:128], Dm[0:TILE, i, 0:m, :], start=True, stop=True)
                for e in range(2):
                    mm = pe.matmul(bk[64 * e:64 * e + 64, 256:256 + m * S // 2], xn[0:TILE, i, 128:D], Dm[0:TILE, i, 0:m, e::2],
                                   start=True, stop=True)
                mm.then_inc(sg["y_ps"], 1)
            pe.wait_ge(sg["L_nrm"], 1)
            for i in range(NT):
                mm = pe.transpose(bank[6 + i // 3][0:S, (i % 3) * TILE:(i % 3) * TILE + TILE], Le[0:TILE, i, :], ident[0:TILE, 0:TILE])
                if i % 3 == 2:
                    mm.then_inc(sg["C_ps"], 1)
            pe.wait_ge(sg["C_sb"], 2)
            for i in range(NT):
                r = rows_of(i)
                if i >= 2:
                    pe.wait_ge(sg["h1b_sb"], i - 1)
                pe.matmul(bank[2 + i % 2][0:r, 0:D], C[0:S, i * TILE:i * TILE + r], b2s[0:S, :], start=True, stop=True)\
                    .then_inc(sg["cb_ps"], 1)

            def fc1(n, r, u, k_before, ring_round):
                pe.wait_ge(sg["ys_sb"], n + 1)
                pe.wait_ge(ld_b1[u], k_before)
                pe.wait_ge(ld_w1[r], ring_round)
                for q in range(2):
                    cols = slice(q * 384, q * 384 + 384)
                    pe.matmul(bank[q][:, 0:384], ind4, b1g[0:GS, u, cols], start=True, stop=False, skip_group_check=True)
                    for k in range(2):
                        for j in range(GS):
                            w = w1a(r)[:, j, cols] if k == 0 else w1b(r)[:, j // 2, cols]
                            mm = pe.matmul(bank[q][32 * j:32 * j + 32, 0:384], ys[:, u, k, j, :], w, start=False,
                                           stop=(k == 1), skip_group_check=True)
                    mm.then_inc(sg["g1_ps"], 1)

            def fc2(n, r, u, ring_round):
                pe.wait_ge(sg["gelu_sb"], 2 * n + 2)
                for c in range(6):
                    mm = pe.transpose(bank[2 + c // 3][:, (c % 3) * 128:(c % 3) * 128 + 128], hg[:, u, c::6], ident)
                    if c % 3 == 2:
                        mm.then_inc(sg["hT_ps"], 1)
                pe.wait_ge(ld_w2[r], ring_round)
                for c in range(6):
                    if c % 3 == 0:
                        pe.wait_ge(sg["hT_sb"], 2 * n + c // 3 + 1)
                    for j in range(GS):
                        mm = pe.matmul(bank[4 + u][32 * j:32 * j + 32, 0:D], hT[:, u, c, 32 * j:32 * j + 32], w2r(r)[:, j, c, :],
                                       start=(c == 0), stop=(c == 5))
                mm.then_inc(sg["y2_ps"], 1)

            pe.wait_ge(sg["h1b_sb"], NT)
            pe.wait_ge(sg["y_sb"], 3 * NT)
            with pe.Fori(0, NG // RING) as i:
                for r in range(RING):
                    n = i * RING + r
                    fc1(n, r, r % 2, 32 * i + 16 * (r // 2 + 1), 48 * i + 48)
                    fc2(n, r, r % 2, 16 * i + 16)
            for u in range(2):
                pe.wait_ge(y_ld[u], 16 * S // 2)
            pe.wait_ge(sg["y2_sb"], NG)
            for q in range(4):
                for x in range(2):
                    for e in range(2):
                        b = 4 * q + 2 * x + e
                        mm = pe.matmul(bank[q][64 * e:64 * e + T, x * D:x * D + D], C[0:S, b * T:b * T + T], Y[0:S, b, :],
                                       start=True, stop=True)
                mm.then_inc(sg["o_ps"], 1)


_ORDER = ["xT", "wT", "cst", "L0_tok_b", "L0_attn_w_attn", "L0_attn_b_attn", "L0_attn_w_proj", "L0_attn_b_proj",
          "L0_attn_w_mem", "L0_attn_b_mem", "L0_attn_w_alpha", "L0_attn_b_alpha", "memT", "L0_ffn_slots",
          "L0_ffn_scale", "L0_ffn_fc1_weight", "L0_ffn_fc1_bias", "L0_ffn_fc2_weight", "L0_ffn_fc2_bias",
          "L0_ffn_norm_weight"]


def constants():
    n = np.arange(8)
    dct = np.sqrt(2.0 / 8) * np.cos(np.pi * (2 * n[None, :] + 1) * n[:, None] / 16)
    dct[0] /= np.sqrt(2.0)
    p = np.arange(128)
    c = np.zeros((128, NCST), np.float32)
    c[:, C_ID:C_ID + 128] = np.eye(128)
    c[:, C_G:C_G + 128] = np.kron(dct, np.kron(np.eye(2), dct))
    c[:GS, C_IND:C_IND + 128] = p[None, :] // 32 == np.arange(GS)[:, None]
    c[:, C_MK:C_MK + HH] = p[:, None] // DH == np.arange(HH)[None, :]
    c[:, C_MV:C_MV + 3] = p[:, None] // T == np.arange(3)[None, :]
    return c


def kernel(**inputs):
    import concourse.bacc as bacc
    from concourse.bass_utils import run_bass_kernel_spmd

    a = {k: np.asarray(v) for k, v in inputs.items()}
    a["xT"] = a["x"].reshape(B, 3, 6, 2, 8, 6, 16).transpose(4, 6, 1, 3, 0, 2, 5).reshape(128, 6 * NTOK)
    a["wT"] = a["L0_tok_w"].reshape(D, 3, 2, 8, 16).transpose(3, 4, 1, 2, 0).reshape(128, 6 * D)
    a["memT"] = a["L0_attn_memory_features"][0].T
    a["cst"] = constants()
    nc = bacc.Bacc("TRN2", target_bir_lowering=False, num_devices=1)
    arrays, args = {}, []
    for name in _ORDER:
        v = np.ascontiguousarray(a[name])
        arrays[f"in_{name}"] = v
        args.append(nc.dram_tensor(f"in_{name}", v.shape, mybir.dt.from_np(v.dtype), kind="ExternalInput").ap())
    args.append(nc.dram_tensor("out_0", (B, T, D), F32, kind="ExternalOutput").ap())
    vit_tower(nc, *args)
    return run_bass_kernel_spmd(nc, [arrays], core_ids=[0]).results[0]["out_0"]
```

```python
from contextlib import ExitStack

import numpy as np

import concourse.bass as bass
from concourse import mybir

F32 = mybir.dt.float32
ALU = mybir.AluOpType
ACT = mybir.ActivationFunctionType
AX = mybir.AxisListType

B, T, D = 16, 36, 192
NTOK = B * T
TILE = 3 * T
NT = 6
PADTOK = NT * TILE
H, DH, M = 12, 16, 100
HD = D // 2
HH = H // 2
S, F = 64, 768
GS = 4
NG = S // GS
RING = 4
BP = 32
EPS = 1e-5

C_ID, C_G, C_IND, C_MK, C_MV, NCST = 0, 128, 256, 384, 390, 393


def rows_of(i):
    return TILE if i < NT - 1 else NTOK - TILE * (NT - 1)


def mrows(i):
    return min(128, NTOK - 128 * i)


def imgs_of(i):
    return rows_of(i) // T


def vit_tower(nc, xT_d, wT_d, cst_d, tok_b, w_attn, b_attn, w_proj, b_proj, w_mem, b_mem, w_alpha, b_alpha,
              memT_d, slots, scale, w1, b1, w2, b2, norm_w, out):
    with ExitStack() as ctx:
        def sb(name, n):
            return ctx.enter_context(nc.sbuf_tensor(name, [128, n], F32))

        def sem(name):
            return ctx.enter_context(nc.semaphore(name))

        GW = GS * F + (GS // 2) * F + GS * (F // 128) * D
        ring = sb("ring", RING * GW)
        front = sb("front", 11648)
        h = sb("h", NT * D)[:, :].rearrange("p (i d) -> p i d", i=NT)
        cst = sb("cst", NCST)
        tokb = sb("tokb", D)
        normb = sb("normb", D)
        a1buf = sb("a1buf", 2 * NTOK)
        a1T = a1buf[:, :].rearrange("p (k t) -> p k t", k=2)
        Vs = a1buf[:, :].rearrange("p (i d) -> p i d", i=NT)
        y2 = a1buf[:, 0:RING * D].rearrange("p (u n) -> p u n", u=RING)
        C = sb("C", PADTOK)
        stats = sb("stats", NT * 8)[:, :].rearrange("p (i c) -> p i c", i=NT)
        small = sb("small", 300)

        def w1a(r):
            return ring[:, r * GW:r * GW + GS * F].rearrange("p (s n) -> p s n", s=GS)

        def w1b(r):
            o = r * GW + GS * F
            return ring[:, o:o + GS // 2 * F].rearrange("p (s n) -> p s n", s=GS // 2)

        def w2r(r):
            o = r * GW + GS * F + GS // 2 * F
            return ring[:, o:(r + 1) * GW].rearrange("p (s c n) -> p s c n", s=GS, c=F // 128)

        def late(o, n):
            o += (RING - 1) * GW
            return ring[:, o:o + n]

        xT = late(0, 3456).rearrange("p (c t) -> p c t", c=6)
        wT = late(3456, 1152)
        weff = late(4608, 1152).rearrange("p (c o) -> p c o", c=6)
        Vb = late(0, 3072).rearrange("p (b n) -> p b n", b=B)
        Kb = late(3072, 1728).rearrange("p (b k n) -> p b k n", b=4, k=2)
        P1 = late(4800, 1800).rearrange("p (u n) -> p u n", u=3)
        P1T = late(6600, 1536).rearrange("p (u h t) -> p u h t", u=2, h=HH)
        Ps = late(8136, 864).rearrange("p (u n) -> p u n", u=2)

        def fr(o, n):
            return front[:, o:o + n]

        wA = fr(0, 1152).rearrange("p (k n) -> p k n", k=2)
        wM = fr(1152, 768).rearrange("p (k n) -> p k n", k=2)
        xlT = fr(1920, 1296).rearrange("p (k t) -> p k t", k=2)
        qT = fr(3216, 1216).rearrange("p (k t) -> p k t", k=2)
        kT = fr(4432, 1152).rearrange("p (k t) -> p k t", k=2)
        wAl = fr(5584, 768).rearrange("p (k n) -> p k n", k=4)
        wP = fr(6352, 384).rearrange("p (k n) -> p k n", k=2)
        memT = fr(6736, 200).rearrange("p (k n) -> p k n", k=2)
        PT = fr(6936, 1024).rearrange("p (u g n) -> p u g n", u=2, g=4)
        am = fr(7960, 384).rearrange("p (u n) -> p u n", u=2)
        aT = fr(8344, 1152).rearrange("p (k t) -> p k t", k=2)
        MKb = fr(9496, 1200).rearrange("p (k n) -> p k n", k=2)
        MVz = fr(10696, 384).rearrange("p (h n) -> p h n", h=H)
        th = fr(0, 1152).rearrange("p (k t) -> p k t", k=2)
        sm = fr(1152, 1152).rearrange("p (k t) -> p k t", k=2)
        df = fr(2304, 1152).rearrange("p (k t) -> p k t", k=2)
        fT = fr(3456, 1152).rearrange("p (k t) -> p k t", k=2)
        hn = fr(6736, 1152).rearrange("p (i d) -> p i d", i=NT)
        hnT = fr(9496, 1296).rearrange("p (k t) -> p k t", k=2)
        L = fr(5584, 384).rearrange("p (i s) -> p i s", i=NT)
        Le = fr(5968, 384).rearrange("p (i s) -> p i s", i=NT)
        LTe = fr(7888, 648)
        Dm = fr(8960, 1152).rearrange("p (i b s) -> p i b s", i=NT, b=3)
        yA = fr(10112, 1024).rearrange("p (s b) -> p s b", s=S)
        yB = fr(11136, 512).rearrange("p (s b) -> p s b", s=S // 2)
        hg = fr(0, 1536).rearrange("p (u n) -> p u n", u=2)
        hT = fr(1536, 1536).rearrange("p (u c m) -> p u c m", u=2, c=6)
        b1f = fr(3072, 1536).rearrange("p (u n) -> p u n", u=2)
        ys = fr(4608, 512).rearrange("p (u w j b) -> p u w j b", u=2, w=2, j=GS)
        Y = fr(5504, 3072).rearrange("p (b n) -> p b n", b=B)
        h1p = fr(8576, 1536).rearrange("p (i d) -> p i d", i=B // 2)

        xl = sb("xl", 2 * D)[:, :].rearrange("p (u d) -> p u d", u=2)
        bnst, epsc, b2s = sb("bnst", 12), sb("epsc", 1), sb("b2s", D)
        slr, squares = fr(11080, D), fr(11272, D)
        slT = fr(11464, 2 * S).rearrange("p (k s) -> p k s", k=2)

        ident = cst[:, C_ID:C_ID + 128]
        dct = cst[:, C_G:C_G + 128]
        b1g = [b1f[64 * (r // 2):64 * (r // 2) + GS, r % 2, :] for r in range(RING)]
        ind4 = [cst[64 * (r // 2):64 * (r // 2) + GS, C_IND:C_IND + 128] for r in range(RING)]
        mask_k = cst[0:HD, C_MK:C_MK + HH]
        mask_v = cst[0:TILE, C_MV:C_MV + 3]

        bank = [ctx.enter_context(nc.psum_tensor(f"bank{i}", [128, 512], F32)) for i in range(8)]

        ld_cst, ld_wT, ld_x0, ld_x1, ld_mem, ld_attn, ld_rows, ld_late = (sem("ld_" + n) for n in (
            "cst", "wT", "x0", "x1", "mem", "attn", "rows", "late"))
        ld_w1 = [sem(f"ld_w1_{r}") for r in range(RING)]
        ld_w2 = [sem(f"ld_w2_{r}") for r in range(RING)]
        ld_b1 = [sem(f"ld_b1_{r}") for r in range(RING)]
        y_ld = [sem(f"y_ld_{u}") for u in range(RING)]
        y_last = sem("y_last")
        filled = sem("filled")
        dve = sem("dve_chain")
        act = sem("act_chain")
        pool = sem("pool_chain")
        names = ("weff_ps weff_sb h_ps h_sb var_sb std_sb xl_sb xlT_ps xlT_sb qk_ps q_sb k_sb v_ps v_sb v_ld v_mask mk_ps mk_sb "
                 "mv_ps mv_sb sl_std sl_sb slT_ps slT_sb kb_sb s1_ps p1_max p1_exp p1_rec p1_norm p1T_ps p1T_sb "
                 "a1T_ps a1T_sb s_ps p_sub p_exp pT_ps pT_sb av_ps a_sb aT_ps aT_sb al_ps th_sb sumdif fT_sb pr_ps h1_sb "
                 "hn_sb ss_sb hnT_ps hnT_sb G_ps veps std2 ms2 rms L_sb LT_ps LT_sub LT_exp LT_nrm Lc_sub Lc_exp Lc_nrm D_ps D_sb "
                 "y_ps yA_sb yB_sb C_ps C_sb cb_ps h1b_sb h1p_ld "
                 "ys_sb g1_ps gelu_sb hT_ps hT_sb y2_ps y2_sb o_ps o_sb stored").split()
        sg = {n: sem(n) for n in names}

        PRB = (7, 0, 4, 5, 6, 7)
        X = small[:, 0:84]
        smask = small[:, 90:108].rearrange("p (i b) -> p i b", i=NT)

        block = ctx.enter_context(nc.Block())
        NB = B // 2
        NM = -(-NTOK // 128)
        NU = 2 * NM
        STEPS = NU + 3
        NHALF = NTOK // 2
        CHUNKS = ((0, NHALF), (NHALF, 512), (512, NTOK))
        CHUNK_PAIRS = (NB // 2, NB, NB)
        CHUNK_UNITS = (6, 8, NU)

        def last_answers(eng, first):
            eng.wait_ge(sg["y2_sb"], NG)
            for j in range(first, first + 2):
                s = S - GS + j
                eng.dma_start(Y[s:s + 1, :, :], y2[32 * j:32 * j + B, RING - 1, :]).then_inc(y_last, 16)

        @block.sync
        def _(sp):
            sp.dma_start(cst[:, :], cst_d).then_inc(ld_cst, 16)
            sp.dma_start(wT, wT_d).then_inc(ld_wT, 16)
            xv = xT_d.rearrange("p (c t) -> p c t", c=6)
            sp.dma_start(xT[:, :, 0:3 * TILE], xv[:, :, 0:3 * TILE]).then_inc(ld_x0, 16)
            sp.dma_start(xT[:, :, 3 * TILE:NTOK], xv[:, :, 3 * TILE:NTOK]).then_inc(ld_x1, 16)

            def load_w1(g, r):
                sp.dma_start(w1a(r), w1[bass.ds(g * GS, GS), 0:128, :].rearrange("s p n -> p s n")).then_inc(ld_w1[r], 16)
                v = w1[bass.ds(g * GS, GS), 128:D, :].rearrange("(q e) p n -> e p q n", e=2)
                for e in range(2):
                    sp.dma_start(w1b(r)[64 * e:64 * e + 64], v[e]).then_inc(ld_w1[r], 16)

            def load_w2(g, r):
                sp.dma_start(w2r(r), w2[bass.ds(g * GS, GS), :, :].rearrange("s (p c) n -> p s c n", c=6)).then_inc(ld_w2[r], 16)

            sp.wait_ge(ld_late, 80)
            for r in range(2):
                load_w1(r, r)
                load_w2(r, r)
            sp.wait_ge(sg["v_sb"], NT)
            for r in range(3):
                for b in range(3):
                    m = NT - (b > 0)
                    sp.dma_start(Vb[T * r:T * r + T, b:b + 3 * (m - 1) + 1:3, :], Vs[T * b:T * b + T, 0:m, :]).then_inc(sg["v_ld"], 16)
            load_w1(2, 2)
            load_w2(2, 2)
            sp.wait_ge(sg["av_ps"], NB)
            load_w1(3, 3)
            sp.wait_ge(sg["a1T_sb"], NU)
            load_w2(3, 3)
            sp.wait_ge(sg["g1_ps"], 2)
            load_w1(RING, 0)
            with sp.Fori(1, NG // RING - 1) as i:
                for r in range(RING):
                    q = r + 1
                    sp.wait_ge(sg["g1_ps"], (i - 1) * (2 * RING) + (2 * q + 2))
                    load_w1(i * RING + q, q % RING)
                    sp.wait_ge(sg["y2_ps"], (i - 1) * RING + (r + 1))
                    load_w2(i * RING + r, r)
            for r in range(RING):
                g = NG - RING + r
                if r < RING - 1:
                    sp.wait_ge(sg["g1_ps"], 2 * (g + 1 - RING) + 2)
                    load_w1(g + 1, r + 1)
                sp.wait_ge(sg["y2_ps"], g - RING + 1)
                load_w2(g, r)

            last_answers(sp, 0)
            ov = out.rearrange("(i e) t d -> e t i d", e=2)
            for q in range(4):
                sp.wait_ge(sg["o_sb"], q + 1)
                for e in range(2):
                    sp.dma_start(ov[e][:, 2 * q:2 * q + 2, :], h1p[64 * e:64 * e + T, 2 * q:2 * q + 2, :]).then_inc(sg["stored"], 16)
            sp.wait_ge(sg["stored"], 8 * 16)

        @block.gpsimd
        def _(gp):
            ended = {}

            def alone(ins, ready=pool):
                ended[ready.name] = ended.get(ready.name, 0) + 1
                ins.then_inc(ready, 1)
                gp.wait_ge(ready, ended[ready.name])

            alone(gp.memset(memT[96:97, 1, :], 1.0), filled)
            alone(gp.memset(epsc[:, :], EPS), filled)
            alone(gp.memset(MVz[:, :, :], 0.0), filled)
            alone(gp.memset(h[:, NT - 1, :], 0.0), filled)
            alone(gp.memset(xlT[96:97, :, :], 1.0), filled)
            alone(gp.memset(qT[:, :, NTOK:608], 0.0), filled)
            alone(gp.memset(qT[96:128, :, 0:NTOK], 0.0), filled)
            alone(gp.memset(MKb[96:128, :, :], 0.0), filled)
            alone(gp.memset(P1T[96:128, :, :, :], 0.0), filled)
            alone(gp.memset(aT[96:97, 1, :], 1.0), filled)

            def k_blocks(i):
                if i >= 2:
                    gp.wait_ge(sg["s_ps"], i - 1)
                for k in range(2):
                    b = 2 * i
                    alone(gp.tensor_tensor(
                        Kb[0:HD, b % 4:b % 4 + 2, k, :].rearrange("p e (h t) -> p e h t", h=HH),
                        kT[0:HD, k, b * T:b * T + 2 * T].rearrange("p (e t) -> p e t", e=2).unsqueeze(2).broadcast_to([HD, 2, HH, T]),
                        mask_k.unsqueeze(1).unsqueeze(3).broadcast_to([HD, 2, HH, T]), ALU.mult), sg["kb_sb"] if k == 1 else pool)

            def sum_and_difference(n):
                gp.wait_ge(sg["aT_sb"], CHUNK_PAIRS[n])
                gp.wait_ge(sg["a1T_sb"], CHUNK_UNITS[n])
                c = slice(*CHUNKS[n])
                alone(gp.tensor_tensor(df[0:HD, :, c], aT[0:HD, :, c], a1T[0:HD, :, c], ALU.subtract), sg["sumdif"])
                alone(gp.tensor_tensor(sm[0:HD, :, c], aT[0:HD, :, c], a1T[0:HD, :, c], ALU.add), sg["sumdif"])

            gp.wait_ge(ld_cst, 16)
            gp.wait_ge(sg["k_sb"], 2)
            k_blocks(0)
            k_blocks(1)
            for n in range(NU):
                if n + 2 == NB // 2:
                    gp.wait_ge(sg["k_sb"], 4)
                if n + 2 < NB:
                    k_blocks(n + 2)
                if n == NU - 1:
                    gp.wait_ge(sg["s_ps"], NB)
                    sum_and_difference(0)
                r = mrows(n // 2)
                gp.wait_ge(sg["p1_rec"], n + 1)
                v = P1[0:r, n % 3, :].rearrange("p (h m) -> p h m", h=HH)
                alone(gp.tensor_tensor(v, v, small[0:r, 24 * (n % 3) + 12:24 * (n % 3) + 18].unsqueeze(2).broadcast_to([r, HH, M]),
                                       ALU.mult), sg["p1_norm"])

            gp.wait_ge(sg["s1_ps"], 2 * NU)
            alone(gp.memset(fT[96:97, 1, :], 2.0), filled)
            sum_and_difference(1)
            sum_and_difference(2)
            gp.wait_ge(sg["al_ps"], 5)
            alone(gp.memset(LTe[0:S, NTOK:PADTOK], 0.0), filled)

            gp.wait_ge(sg["C_ps"], 2)
            for g in range(NG - 1):
                gp.wait_ge(sg["y2_sb"], g + 1)
                for j in range(GS):
                    s = g * GS + j
                    gp.dma_start(Y[s:s + 1, :, :], y2[32 * j:32 * j + B, g % RING, :]).then_inc(y_ld[g % RING], 16)
                if g < B // 2:
                    gp.wait_ge(sg["h1b_sb"], NT)
                    for b in range(2 * g, 2 * g + 2):
                        p = T * (b % 3)
                        q = 64 * (b % 2)
                        gp.dma_start(h1p[q:q + T, b // 2, :], h[p:p + T, b // 3, :]).then_inc(sg["h1p_ld"], 16)

        @block.scalar
        def _(sc):
            half = "(k p) n -> p k n"
            sc.dma_start(memT[0:HD], memT_d.rearrange(half, k=2)).then_inc(ld_mem, 16)
            sc.dma_start(wM[0:HD], w_mem.rearrange(half, k=2)).then_inc(ld_mem, 16)
            sc.dma_start(wM[96:97, 1, :], b_mem.unsqueeze(0)).then_inc(ld_mem, 16)
            sc.dma_start(tokb[:, :], tok_b.unsqueeze(0).broadcast_to([128, D])).then_inc(ld_rows, 16)
            sc.dma_start(normb[:, :], norm_w.unsqueeze(0).broadcast_to([128, D])).then_inc(ld_rows, 16)
            sc.dma_start(slr[0:S, :], slots).then_inc(ld_rows, 16)
            sc.dma_start(small[0:S, 299:300], scale.unsqueeze(1)).then_inc(ld_rows, 16)
            sc.dma_start(wA[0:HD], w_attn.rearrange(half, k=2)).then_inc(ld_attn, 16)
            sc.dma_start(wA[96:97, 1, :], b_attn.unsqueeze(0)).then_inc(ld_attn, 16)
            sc.dma_start(wAl[0:HD], w_alpha.rearrange("(k p) n -> p k n", k=4)).then_inc(ld_late, 16)
            sc.dma_start(wAl[96:97, 1, :], b_alpha.unsqueeze(0)).then_inc(ld_late, 16)
            sc.dma_start(wP[0:HD], w_proj.rearrange(half, k=2)).then_inc(ld_late, 16)
            sc.dma_start(wP[96:97, 1, :], b_proj.unsqueeze(0)).then_inc(ld_late, 16)
            sc.dma_start(b2s[0:S, :], b2).then_inc(ld_late, 16)

            def xlT_copy(i):
                sc.wait_ge(sg["xlT_ps"], i + 1)
                n = rows_of(i)
                sc.activation(xlT[0:HD, :, i * TILE:i * TILE + n],
                              bank[1 + i % 2][0:HD, 0:2 * TILE].rearrange("p (k t) -> p k t", k=2)[:, :, 0:n], ACT.Copy)\
                    .then_inc(sg["xlT_sb"], 1)

            sc.wait_ge(ld_rows, 64)
            sc.activation(squares[0:S, :], slr[0:S, :], ACT.Square, accum_out=small[0:S, 290:291]).then_inc(act, 1)
            sc.wait_ge(act, 1)
            sc.activation(small[0:S, 291:292], small[0:S, 290:291], ACT.Sqrt).then_inc(sg["sl_std"], 1)
            for i in range(NT):
                sc.wait_ge(sg["var_sb"], i + 1)
                sc.activation(stats[0:TILE, i, 3:4], stats[0:TILE, i, 2:3], ACT.Sqrt).then_inc(sg["std_sb"], 1)
                if i >= 1:
                    xlT_copy(i - 1)
            xlT_copy(NT - 1)
            sc.activation(small[0:S, 294:295], small[0:S, 290:291], ACT.Exp, scale=0.0)
            for u in range(4):
                n, m = divmod(u, 2)
                sc.wait_ge(sg["qk_ps"], 4 * n + m + 3)
                sc.activation(qT[0:HD, m, n * NHALF:(n + 1) * NHALF], bank[((5, 7), (5, 6))[n][m]][0:HD, 0:NHALF], ACT.Copy)\
                    .then_inc(sg["q_sb"], 1)

            def tanh(n, m):
                sc.wait_ge(sg["al_ps"], 2 * n + m + 1)
                c = slice(*CHUNKS[n])
                sc.activation(th[0:HD, m, c], bank[2 * n + m][0:HD, 0:c.stop - c.start], ACT.Tanh, scale=0.5).then_inc(sg["th_sb"], 1)

            def tanh_last():
                sc.wait_ge(sg["al_ps"], 5)
                c = slice(*CHUNKS[2])
                sc.activation(th[0:HD, :, c], bank[1][0:HD, :].rearrange("p (k t) -> p k t", k=2)[:, :, 0:c.stop - c.start],
                              ACT.Tanh, scale=0.5).then_inc(sg["th_sb"], 1)

            def hnT_copy(i):
                sc.wait_ge(sg["hnT_ps"], i + 1)
                sc.activation(hnT[0:HD, :, i * TILE:(i + 1) * TILE],
                              bank[i % 2][0:HD, 0:2 * TILE].rearrange("p (k t) -> p k t", k=2), ACT.Copy).then_inc(sg["hnT_sb"], 1)

            sc.wait_ge(filled, 9)
            for n in range(STEPS):
                if 0 <= n - 2 < NB:
                    u = n - 2
                    sc.wait_ge(sg["pT_ps"], u + 1)
                    if u >= 2:
                        sc.wait_ge(sg["av_ps"], u - 1)
                    sc.activation(PT[0:TILE, u % 2, :, :], bank[1][0:TILE, :].rearrange("p (g m) -> p g m", g=4), ACT.Copy)\
                        .then_inc(sg["pT_sb"], 1)
                if n < NB:
                    sc.wait_ge(sg["p_sub"], n + 1)
                    sc.activation(Ps[:, n % 2, :], Ps[:, n % 2, :], ACT.Exp).then_inc(sg["p_exp"], 1)
                if n < NU:
                    r = mrows(n // 2)
                    o = 24 * (n % 3)
                    for x in range(HH):
                        if x % 3 == 0:
                            sc.wait_ge(sg["p1_max"], 2 * n + x // 3 + 1)
                        if x == 0 and n >= 3:
                            sc.wait_ge(sg["p1T_ps"], n - 2)
                        e = sc.activation(P1[0:r, n % 3, x * M:x * M + M], bank[2 + x // 3][0:r, (x % 3) * M:(x % 3) * M + M], ACT.Exp,
                                          bias=small[0:r, o + x:o + x + 1], accum_out=small[0:r, o + 6 + x:o + 7 + x])
                        if x % 3 == 2:
                            e.then_inc(sg["p1_exp"], 1)
                if 0 <= n - 3 < NU:
                    u = n - 3
                    i, k = divmod(u, 2)
                    r = mrows(i)
                    sc.wait_ge(sg["a1T_ps"], u + 1)
                    if u == 0:
                        sc.wait_ge(sg["v_ld"], 16 * 9)
                    sc.activation(a1T[0:HD, k, i * 128:i * 128 + r], bank[6][0:HD, 0:r], ACT.Copy).then_inc(sg["a1T_sb"], 1)
                if 0 <= n - 2 < NU:
                    u = n - 2
                    r = mrows(u // 2)
                    sc.wait_ge(sg["p1T_ps"], u + 1)
                    if u >= 2:
                        sc.wait_ge(sg["a1T_ps"], u - 1)
                    for q in range(2):
                        ins = sc.activation(P1T[0:M, u % 2, 3 * q:3 * q + 3, 0:r],
                                            bank[4 + q][0:M, 0:384].rearrange("p (h t) -> p h t", h=3)[:, :, 0:r], ACT.Copy)
                    ins.then_inc(sg["p1T_sb"], 1)
                if 0 <= n - 3 < NB:
                    u = n - 3
                    sc.wait_ge(sg["aT_ps"], u + 1)
                    for k in range(2):
                        ins = sc.activation(aT[0:HD, k, 2 * T * u:2 * T * (u + 1)].rearrange("p (e t) -> p e t", e=2),
                                            bank[4 + k][0:HD, 384:512].rearrange("p (e t) -> p e t", e=2)[:, :, 0:T], ACT.Copy)
                    ins.then_inc(sg["aT_sb"], 1)
                if n in (NU, NU + 1):
                    tanh(0, n - NU)
            tanh(1, 0)
            tanh(1, 1)
            tanh_last()

            for i in range(NT):
                if i == 2:
                    sc.activation(small[0:S, 295:296], small[0:S, 290:291], ACT.Sqrt, scale=0.0)
                sc.wait_ge(sg["hn_sb"], i + 1)
                if i >= 2:
                    sc.wait_ge(sg["ss_sb"], i - 1)
                sc.activation(xl[0:TILE, i % 2, :], hn[0:TILE, i, :], ACT.Square, accum_out=X[0:TILE, 6 + i:7 + i]).then_inc(sg["ss_sb"], 1)
                if i >= 1:
                    hnT_copy(i - 1)
            hnT_copy(NT - 1)
            sc.wait_ge(sg["veps"], 1)
            sc.wait_ge(sg["ss_sb"], NT)
            sc.activation(X[0:TILE, 12:24], X[0:TILE, 0:12], ACT.Sqrt).then_inc(sg["std2"], 1)
            sc.wait_ge(sg["ms2"], 1)
            sc.activation(X[0:TILE, 36:42], X[0:TILE, 30:36], ACT.Sqrt, bias=epsc[0:TILE, 0:1]).then_inc(sg["rms"], 1)
            def biases(g, r):
                sc.dma_start(b1g[r], b1[bass.ds(g * GS, GS), :]).then_inc(ld_b1[r], 16)

            for r in range(RING):
                biases(r, r)
            sc.wait_ge(sg["LT_sub"], 1)
            sc.activation(LTe[0:S, 0:NTOK], LTe[0:S, 0:NTOK], ACT.Exp).then_inc(sg["LT_exp"], 1)
            sc.wait_ge(sg["Lc_sub"], 1)
            sc.activation(Le[0:TILE], Le[0:TILE], ACT.Exp).then_inc(sg["Lc_exp"], 1)
            for i in range(NT):
                m = imgs_of(i)
                sc.wait_ge(sg["y_ps"], i + 1)
                for e in range(2):
                    p = slice(64 * e, 64 * e + 64)
                    sc.activation(yB[p, :, 3 * i:3 * i + m].rearrange("p s b -> p b s"),
                                  bank[i % 2][p, 0:m * S // 2].rearrange("p (b s) -> p b s", b=m), ACT.Copy)\
                        .then_inc(sg["yB_sb"], 1)

            def gelu(n, u):
                for q in range(2):
                    sc.wait_ge(sg["g1_ps"], n * 2 + q + 1)
                    sc.activation(hg[:, u, q * 384:q * 384 + 384], bank[q][:, 0:384], ACT.Gelu).then_inc(sg["gelu_sb"], 1)

            with sc.Fori(0, NG // RING - 1) as i:
                for r in range(RING):
                    gelu(i * RING + r, r % 2)
                    biases(i * RING + (r + RING), r)
            for r in range(RING):
                gelu((NG // RING - 1) * RING + r, r % 2)
            last_answers(sc, 2)

        @block.vector
        def _(ve):
            chain = [0]

            def link(ins):
                chain[0] += 1
                ins.then_inc(dve, 1)
                ve.wait_ge(dve, chain[0])

            for q in range(3):
                ve.wait_ge(sg["weff_ps"], q + 1)
                ve.tensor_copy(weff[:, 2 * q:2 * q + 2, :], bank[q][:, 0:384].rearrange("p (c o) -> p c o", c=2))\
                    .then_inc(sg["weff_sb"], 1)
            ve.wait_ge(ld_cst, 16)
            ve.wait_ge(sg["mk_ps"], 1)
            for k in range(2):
                ins = ve.tensor_tensor(MKb[0:HD, k, :].rearrange("p (h m) -> p h m", h=HH),
                                       bank[5][0:HD, k * M:k * M + M].unsqueeze(1).broadcast_to([HD, HH, M]),
                                       mask_k.unsqueeze(2).broadcast_to([HD, HH, M]), ALU.mult)
            ins.then_inc(sg["mk_sb"], 1)
            ve.wait_ge(sg["mv_ps"], 1)
            ve.wait_ge(filled, 3)
            for e in range(2):
                ins = ve.tensor_copy(MVz[0:M, e::2, DH * e:DH * e + DH],
                                     bank[6][0:M, 0:D].rearrange("p (h e c) -> p h e c", e=2, c=DH)[:, :, e, :])
            ins.then_inc(sg["mv_sb"], 1)
            ve.wait_ge(sg["sl_std"], 1)
            link(ve.tensor_scalar(small[0:S, 292:293], small[0:S, 291:292], EPS, None, ALU.max))
            link(ve.reciprocal(small[0:S, 293:294], small[0:S, 292:293]))
            ve.tensor_scalar(slr[0:S, :], slr[0:S, :], small[0:S, 293:294], small[0:S, 299:300], ALU.mult, ALU.mult)\
                .then_inc(sg["sl_sb"], 1)

            ve.wait_ge(filled, 4)
            for i in range(NT + 1):
                if i < NT:
                    r = rows_of(i)
                    ve.wait_ge(sg["h_ps"], i + 1)
                    link(ve.tensor_tensor(h[0:r, i, :], bank[(3 + i) % 8][0:r, 0:D], tokb[0:r, :], ALU.add))
                    link(ve.bn_stats(bnst[0:TILE, 0:6], h[0:TILE, i, :]))
                    link(ve.bn_aggr(stats[0:TILE, i, 0:2], bnst[0:TILE, 0:6]))
                    ve.tensor_scalar(stats[0:TILE, i, 2:3], stats[0:TILE, i, 1:2], EPS, None, ALU.add).then_inc(sg["var_sb"], 1)
                if i >= 1:
                    j = i - 1
                    ve.wait_ge(sg["std_sb"], i)
                    if i >= 3:
                        ve.wait_ge(sg["xlT_ps"], i - 2)
                    link(ve.reciprocal(stats[0:TILE, j, 4:5], stats[0:TILE, j, 3:4]))
                    ve.tensor_scalar(xl[0:TILE, j % 2, :], h[0:TILE, j, :], stats[0:TILE, j, 0:1], stats[0:TILE, j, 4:5],
                                     ALU.subtract, ALU.mult).then_inc(sg["xl_sb"], 1)
            ve.wait_ge(sg["slT_ps"], 1)
            ve.tensor_copy(slT[0:HD, :, :], bank[6][0:HD, 0:2 * S].rearrange("p (k s) -> p k s", k=2)).then_inc(sg["slT_sb"], 1)
            for u in range(4):
                n, m = divmod(u, 2)
                ve.wait_ge(sg["qk_ps"], 4 * n + m + 1)
                ve.tensor_copy(kT[0:HD, m, n * NHALF:(n + 1) * NHALF], bank[3 + m][0:HD, 0:NHALF]).then_inc(sg["k_sb"], 1)
            for i in range(NT):
                r = rows_of(i)
                ve.wait_ge(sg["v_ps"], i + 1)
                ve.tensor_copy(Vs[0:r, i, :], bank[(7, 0)[i % 2]][0:r, 0:D]).then_inc(sg["v_sb"], 1)

            def fuse(n):
                c = slice(*CHUNKS[n])
                ve.wait_ge(sg["sumdif"], 2 * n + 2)
                ve.wait_ge(sg["th_sb"], (2, 4, 5)[n])
                ve.wait_ge(filled, 11)
                link(ve.tensor_tensor(df[0:HD, :, c], df[0:HD, :, c], th[0:HD, :, c], ALU.mult))
                ve.tensor_tensor(fT[0:HD, :, c], df[0:HD, :, c], sm[0:HD, :, c], ALU.add).then_inc(sg["fT_sb"], 1)

            def residual(i):
                def after(ins):
                    chain[0] += 1
                    ins.then_inc(dve, 1)
                    return chain[0]

                two = (i, i + 1)
                done = []
                for t in two:
                    r = rows_of(t)
                    ve.wait_ge(sg["pr_ps"], t + 1)
                    done.append(after(ve.scalar_tensor_tensor(out=h[0:r, t, :], in0=bank[PRB[t]][0:r, 0:D], scalar=0.5,
                                                              in1=h[0:r, t, :], op0=ALU.mult, op1=ALU.add)))
                for x, t in enumerate(two):
                    ve.wait_ge(dve, done[x])
                    done[x] = after(ve.bn_stats(bnst[0:TILE, 6 * x:6 * x + 6], h[0:TILE, t, :]))
                for x, t in enumerate(two):
                    ve.wait_ge(dve, done[x])
                    done[x] = after(ve.bn_aggr(stats[0:TILE, t, 0:2], bnst[0:TILE, 6 * x:6 * x + 6]))
                for x, t in enumerate(two):
                    ve.wait_ge(dve, done[x])
                    ve.scalar_tensor_tensor(out=hn[0:TILE, t, :], in0=h[0:TILE, t, :], scalar=stats[0:TILE, t, 0:1],
                                            in1=normb[0:TILE, :], op0=ALU.subtract, op1=ALU.mult).then_inc(sg["hn_sb"], 1)

            for n in range(STEPS):
                if 0 <= n - 1 < NU:
                    r = mrows((n - 1) // 2)
                    o = 24 * ((n - 1) % 3)
                    ve.wait_ge(sg["p1_exp"], 2 * n)
                    ve.reciprocal(small[0:r, o + 12:o + 18], small[0:r, o + 6:o + 12]).then_inc(sg["p1_rec"], 1)
                if n < NB:
                    ve.wait_ge(sg["s_ps"], n + 1)
                    if n >= 2:
                        ve.wait_ge(sg["pT_ps"], n - 1)
                    sv = bank[0][:, 0:432].rearrange("p (h t) -> p h t", h=H)
                    mx = small[:, 140 + 36 * (n % 3):152 + 36 * (n % 3)]
                    link(ve.tensor_reduce(mx, sv, AX.X, ALU.max))
                    ve.tensor_tensor(Ps[:, n % 2, :].rearrange("p (h t) -> p h t", h=H), sv,
                                     mx.unsqueeze(2).broadcast_to([128, H, T]), ALU.subtract).then_inc(sg["p_sub"], 1)
                if n < NU:
                    r = mrows(n // 2)
                    for q in range(2):
                        ve.wait_ge(sg["s1_ps"], 2 * n + q + 1)
                        ve.tensor_reduce(small[0:r, 24 * (n % 3) + 3 * q:24 * (n % 3) + 3 * q + 3],
                                         bank[2 + q][0:r, 0:300].rearrange("p (h m) -> p h m", h=3), AX.X, ALU.max, negate=True)\
                            .then_inc(sg["p1_max"], 1)
                if n < NB:
                    o = 140 + 36 * (n % 3)
                    ve.wait_ge(sg["p_exp"], n + 1)
                    link(ve.tensor_reduce(small[:, o + 12:o + 24], Ps[:, n % 2, :].rearrange("p (h t) -> p h t", h=H), AX.X, ALU.add))
                    link(ve.reciprocal(small[:, o + 24:o + 36], small[:, o + 12:o + 24]))
                if 0 <= n - 1 < NB:
                    u = n - 1
                    if u == 0:
                        ve.wait_ge(sg["v_ld"], 16 * 9)
                    v = Vb[0:TILE, 2 * u:2 * u + 2, :].rearrange("p b (g r c) -> p (b g) r c", g=4, r=3)
                    ve.tensor_tensor(v, v, mask_v.unsqueeze(1).unsqueeze(3).broadcast_to([TILE, 8, 3, DH]), ALU.mult)\
                        .then_inc(sg["v_mask"], 1)
                if 0 <= n - 2 < NB:
                    u = n - 2
                    o = 140 + 36 * (u % 3) + 24
                    ve.wait_ge(sg["av_ps"], u + 1)
                    if u >= 2:
                        ve.wait_ge(sg["aT_ps"], u - 1)
                    ve.tensor_tensor(am[:, u % 2, :].rearrange("p (h c) -> p h c", h=H),
                                     bank[7][:, 0:D].rearrange("p (h c) -> p h c", h=H),
                                     small[:, o:o + H].unsqueeze(2).broadcast_to([128, H, DH]), ALU.mult).then_inc(sg["a_sb"], 1)
                if n == NU + 1:
                    fuse(0)
            fuse(1)
            residual(0)
            fuse(2)
            residual(2)
            residual(4)

            link(ve.tensor_copy(X[0:TILE, 24:30], stats[0:TILE, :, 1]))
            ve.tensor_scalar(X[0:TILE, 0:6], X[0:TILE, 24:30], EPS, None, ALU.add).then_inc(sg["veps"], 1)
            ve.wait_ge(sg["veps"], 1)
            link(ve.reciprocal(X[0:TILE, 42:48], X[0:TILE, 0:6]))
            ve.tensor_tensor(X[0:TILE, 30:36], X[0:TILE, 42:48], X[0:TILE, 24:30], ALU.mult).then_inc(sg["ms2"], 1)
            ve.wait_ge(sg["std2"], 1)
            ve.wait_ge(sg["rms"], 1)
            link(ve.tensor_tensor(X[0:TILE, 54:60], X[0:TILE, 36:42], X[0:TILE, 12:18], ALU.mult))
            link(ve.scalar_tensor_tensor(out=X[0:TILE, 66:72], in0=X[0:TILE, 54:60], scalar=EPS, in1=X[0:TILE, 18:24],
                                         op0=ALU.mult, op1=ALU.max))
            link(ve.reciprocal(X[0:TILE, 78:84], X[0:TILE, 66:72]))
            ve.wait_ge(sg["G_ps"], 1)
            ve.tensor_tensor(L[0:TILE], bank[2][0:TILE, 0:384].rearrange("p (i s) -> p i s", i=NT),
                             X[0:TILE, 78:84].unsqueeze(2).broadcast_to([TILE, NT, S]), ALU.mult).then_inc(sg["L_sb"], 1)
            link(ve.reciprocal(X[0:TILE, 60:66], X[0:TILE, 54:60]))
            ve.tensor_tensor(smask[0:TILE], mask_v.unsqueeze(1).broadcast_to([TILE, NT, 3]),
                             X[0:TILE, 60:66].unsqueeze(2).broadcast_to([TILE, NT, 3]), ALU.mult)
            lt = [bank[3 + q][0:S, 0:324].rearrange("p (b t) -> p b t", b=9) for q in range(2)]
            nb = (9, 7)
            for q in range(2):
                ve.wait_ge(sg["LT_ps"], q + 1)
                ins = ve.tensor_reduce(small[0:S, 9 * q:9 * q + nb[q]], lt[q][:, 0:nb[q], :], AX.X, ALU.max)
            link(ins)
            for q in range(2):
                ins = ve.tensor_tensor(LTe[0:S, 324 * q:324 * q + T * nb[q]].rearrange("p (b t) -> p b t", b=nb[q]), lt[q][:, 0:nb[q], :],
                                       small[0:S, 9 * q:9 * q + nb[q]].unsqueeze(2).broadcast_to([S, nb[q], T]), ALU.subtract)
            ins.then_inc(sg["LT_sub"], 1)
            link(ve.tensor_reduce(small[0:TILE, 20:26], L[0:TILE], AX.X, ALU.max))
            ve.tensor_tensor(Le[0:TILE], L[0:TILE], small[0:TILE, 20:26].unsqueeze(2).broadcast_to([TILE, NT, S]), ALU.subtract)\
                .then_inc(sg["Lc_sub"], 1)
            ve.wait_ge(sg["LT_exp"], 1)
            le = LTe[0:S, 0:NTOK].rearrange("p (b t) -> p b t", b=B)
            link(ve.tensor_reduce(small[0:S, 30:46], le, AX.X, ALU.add))
            link(ve.reciprocal(small[0:S, 50:66], small[0:S, 30:46]))
            ve.tensor_tensor(le, le, small[0:S, 50:66].unsqueeze(2).broadcast_to([S, B, T]), ALU.mult).then_inc(sg["LT_nrm"], 1)
            for q in range(2):
                ve.wait_ge(sg["D_ps"], q + 1)
                i = slice(3 * q, 3 * q + 3)
                ve.tensor_tensor(Dm[0:TILE, i],
                                 bank[5 - q][0:TILE, 0:192].rearrange("p (i s) -> p i s", i=3).unsqueeze(2).broadcast_to([TILE, 3, 3, S]),
                                 smask[0:TILE, i].unsqueeze(3).broadcast_to([TILE, 3, 3, S]), ALU.mult).then_inc(sg["D_sb"], 1)
            ve.memset(ys[:, :, :, :, :], 0.0)
            for i in range(NT):
                m = imgs_of(i)
                ve.wait_ge(sg["y_ps"], i + 1)
                ve.tensor_copy(yA[:, :, 3 * i:3 * i + m].rearrange("p s b -> p b s"),
                               bank[6 + i % 2][:, 0:m * S].rearrange("p (b s) -> p b s", b=m)).then_inc(sg["yA_sb"], 1)

            def stationary(g, u):
                ve.tensor_copy(ys[:, u, 0, :, 0:B], yA[:, bass.ds(g * GS, GS), :])
                for e in range(2):
                    p = slice(64 * e, 64 * e + 64)
                    ins = ve.tensor_copy(ys[p, u, 1, e::2, 0:B], yB[p, bass.ds(g * (GS // 2), GS // 2), :])
                ins.then_inc(sg["ys_sb"], 1)

            def hidden(n, u):
                for q in range(2):
                    ve.wait_ge(sg["hT_ps"], 2 * n + (q + 1))
                    ve.tensor_copy(hT[:, u, 3 * q:3 * q + 3, :], bank[2 + q][:, 0:384].rearrange("p (c m) -> p c m", c=3))\
                        .then_inc(sg["hT_sb"], 1)

            def gather(n, r):
                ve.wait_ge(sg["y2_ps"], n + 1)
                ve.tensor_copy(y2[:, r, :], bank[4 + r % 2][:, 0:D]).then_inc(sg["y2_sb"], 1)

            ve.wait_ge(sg["yA_sb"], NT)
            ve.wait_ge(sg["yB_sb"], 2 * NT)
            stationary(0, 0)
            stationary(1, 1)
            ve.wait_ge(sg["Lc_exp"], 1)
            link(ve.tensor_reduce(small[0:TILE, 70:76], Le[0:TILE], AX.X, ALU.add))
            link(ve.reciprocal(small[0:TILE, 80:86], small[0:TILE, 70:76]))
            ve.tensor_tensor(Le[0:TILE], Le[0:TILE], small[0:TILE, 80:86].unsqueeze(2).broadcast_to([TILE, NT, S]), ALU.mult)\
                .then_inc(sg["Lc_nrm"], 1)
            for n in range(RING):
                ve.wait_ge(sg["g1_ps"], 2 * n + 2)
                stationary(n + 2, n % 2)
                hidden(n, n % 2)
                gather(n, n)
                if n == 0:
                    for q in range(2):
                        ve.wait_ge(sg["C_ps"], q + 1)
                        ve.tensor_copy(C[0:S, 324 * q:324 * q + 324], bank[6 + q][0:S, 0:324]).then_inc(sg["C_sb"], 1)
                    for i in range(NT):
                        r = rows_of(i)
                        ve.wait_ge(sg["cb_ps"], i + 1)
                        ve.tensor_tensor(h[0:r, i, :], bank[6 + i % 2][0:r, 0:D], h[0:r, i, :], ALU.add)\
                            .then_inc(sg["h1b_sb"], 1)
            with ve.Fori(1, NG // RING - 1) as i:
                for r in range(RING):
                    n = i * RING + r
                    ve.wait_ge(sg["g1_ps"], i * (2 * RING) + (2 * r + 2))
                    stationary(i * RING + (r + 2), r % 2)
                    hidden(n, r % 2)
                    ve.wait_ge(y_ld[r], 64 * i)
                    gather(n, r)
            for r in range(RING):
                n = NG - RING + r
                if r < 2:
                    ve.wait_ge(sg["g1_ps"], 2 * n + 2)
                    stationary(n + 2, r % 2)
                hidden(n, r % 2)
                ve.wait_ge(y_ld[r], 64 * (n // RING))
                gather(n, r)

            ve.wait_ge(sg["h1p_ld"], 16 * B)
            for q in range(4):
                ve.wait_ge(sg["o_ps"], q + 1)
                for e in range(2):
                    p = slice(64 * e, 64 * e + T)
                    v = h1p[p, 2 * q:2 * q + 2, :]
                    ins = ve.tensor_tensor(v, v, bank[q][p, 0:384].rearrange("p (i d) -> p i d", i=2), ALU.add)
                ins.then_inc(sg["o_sb"], 1)

        @block.tensor
        def _(pe):
            def kr(k):
                return HD + k

            pe.wait_ge(ld_cst, 16)
            pe.wait_ge(ld_wT, 16)
            for q in range(3):
                pe.matmul(bank[q][:, 0:384], dct, wT[:, q * 384:q * 384 + 384], start=True, stop=True).then_inc(sg["weff_ps"], 1)
            pe.wait_ge(ld_mem, 48)
            pe.wait_ge(filled, 1)
            for m in range(2):
                for k in range(2):
                    mm = pe.matmul(bank[5][0:HD, m * M:m * M + M], wM[0:kr(k), k, m * HD:m * HD + HD], memT[0:kr(k), k, :],
                                   start=(k == 0), stop=(k == 1))
            mm.then_inc(sg["mk_ps"], 1)
            for k in range(2):
                mm = pe.matmul(bank[6][0:M, 0:D], memT[0:kr(k), k, :], wM[0:kr(k), k, D:2 * D], start=(k == 0), stop=(k == 1))
            mm.then_inc(sg["mv_ps"], 1)
            pe.wait_ge(ld_x0, 16)
            pe.wait_ge(sg["weff_sb"], 3)

            def xl_transpose(i):
                pe.wait_ge(sg["xl_sb"], i + 1)
                if i >= 2:
                    pe.wait_ge(sg["xlT_sb"], i - 1)
                for k in range(2):
                    mm = pe.transpose(bank[1 + i % 2][0:HD, k * TILE:k * TILE + TILE], xl[0:TILE, i % 2, k * HD:k * HD + HD],
                                      ident[0:TILE, 0:TILE])
                mm.then_inc(sg["xlT_ps"], 1)

            def q_or_k(which, m, n, bk):
                o = which * D + m * HD
                for k in range(2):
                    mm = pe.matmul(bank[bk][0:HD, 0:NHALF], wA[0:kr(k), k, o:o + HD], xlT[0:kr(k), k, n * NHALF:(n + 1) * NHALF],
                                   start=(k == 0), stop=(k == 1))
                mm.then_inc(sg["qk_ps"], 1)

            for i in range(NT):
                r = rows_of(i)
                if i == 2:
                    pe.wait_ge(sg["mk_sb"], 1)
                    pe.wait_ge(sg["mv_sb"], 1)
                if i == 3:
                    pe.wait_ge(ld_x1, 16)
                for c in range(6):
                    mm = pe.matmul(bank[(3 + i) % 8][0:r, 0:D], xT[:, c, i * TILE:i * TILE + r], weff[:, c, :],
                                   start=(c == 0), stop=(c == 5))
                mm.then_inc(sg["h_ps"], 1)
                if i >= 2:
                    xl_transpose(i - 2)
            pe.wait_ge(sg["sl_sb"], 1)
            pe.wait_ge(sg["var_sb"], 4)
            for k in range(2):
                mm = pe.transpose(bank[6][0:HD, k * S:k * S + S], slr[0:S, k * HD:k * HD + HD], ident[0:S, 0:S])
            mm.then_inc(sg["slT_ps"], 1)
            pe.wait_ge(ld_attn, 32)
            pe.wait_ge(filled, 8)
            pe.wait_ge(sg["xlT_sb"], 3)
            q_or_k(1, 0, 0, 3)
            q_or_k(1, 1, 0, 4)
            xl_transpose(NT - 2)
            pe.wait_ge(sg["var_sb"], 5)
            q_or_k(0, 0, 0, 5)
            xl_transpose(NT - 1)
            q_or_k(0, 1, 0, 7)
            pe.wait_ge(sg["xlT_sb"], NT)
            pe.wait_ge(sg["k_sb"], 1)
            q_or_k(1, 0, 1, 3)
            pe.wait_ge(sg["k_sb"], 2)
            q_or_k(1, 1, 1, 4)
            pe.wait_ge(sg["q_sb"], 1)
            q_or_k(0, 0, 1, 5)
            pe.wait_ge(sg["slT_sb"], 1)
            q_or_k(0, 1, 1, 6)
            pe.wait_ge(sg["q_sb"], 2)
            pe.wait_ge(sg["var_sb"], NT)
            for i in range(NT):
                r = rows_of(i)
                if i >= 2:
                    pe.wait_ge(sg["v_sb"], i - 1)
                for k in range(2):
                    mm = pe.matmul(bank[(7, 0)[i % 2]][0:r, 0:D], xlT[0:kr(k), k, i * TILE:i * TILE + r],
                                   wA[0:kr(k), k, 2 * D:3 * D], start=(k == 0), stop=(k == 1))
                mm.then_inc(sg["v_ps"], 1)

            def alpha(n, m, bk, o):
                c = slice(*CHUNKS[n])
                for k in range(4):
                    src = (aT, a1T)[k // 2]
                    rows = HD + (k == 1)
                    mm = pe.matmul(bank[bk][0:HD, o:o + c.stop - c.start], wAl[0:rows, k, m * HD:m * HD + HD],
                                   src[0:rows, k % 2, c], start=(k == 0), stop=(k == 3))
                return mm

            def project(i):
                r = rows_of(i)
                for k in range(2):
                    mm = pe.matmul(bank[PRB[i]][0:r, 0:D], fT[0:kr(k), k, i * TILE:i * TILE + r], wP[0:kr(k), k, :],
                                   start=(k == 0), stop=(k == 1))
                mm.then_inc(sg["pr_ps"], 1)

            pe.wait_ge(sg["q_sb"], 4)
            pe.wait_ge(sg["v_sb"], NT)
            pe.wait_ge(filled, 9)
            for n in range(STEPS):
                if n < NB:
                    pe.wait_ge(sg["kb_sb"], n + 1)
                    if n >= 1:
                        pe.wait_ge(sg["p_sub"], n)
                    for k in range(2):
                        for e in range(2):
                            b = 2 * n + e
                            mm = pe.matmul(bank[0][64 * e:64 * e + 64, 216 * k:216 * k + 216], qT[0:HD, k, b * T:b * T + 64],
                                           Kb[0:HD, b % 4, k, :], start=True, stop=True)
                    mm.then_inc(sg["s_ps"], 1)
                if n < NU:
                    i, k = divmod(n, 2)
                    r = mrows(i)
                    for q in range(2):
                        if n >= 1:
                            pe.wait_ge(sg["p1_exp"], 2 * n - 1 + q)
                        pe.matmul(bank[2 + q][0:r, 0:300], qT[:, k, i * 128:i * 128 + r],
                                  MKb[:, k, 300 * q:300 * q + 300], start=True, stop=True).then_inc(sg["s1_ps"], 1)
                if 0 <= n - 3 < NU:
                    u = n - 3
                    i, k = divmod(u, 2)
                    r = mrows(i)
                    pe.wait_ge(sg["p1T_sb"], u + 1)
                    if u >= 1:
                        pe.wait_ge(sg["a1T_sb"], u)
                    for par in range(2):
                        for c in range(3):
                            x = 2 * c + par
                            mm = pe.matmul(bank[6][32 * c:32 * c + 32, 0:r], MVz[:, k * HH + x, :], P1T[:, u % 2, x, 0:r],
                                           start=(par == 0), stop=(par == 1))
                    mm.then_inc(sg["a1T_ps"], 1)
                if n >= 3:
                    pe.wait_ge(sg["p1T_sb"], min(n - 2, NU))
                if n >= 4:
                    pe.wait_ge(sg["aT_sb"], min(n - 3, NB))
                if 0 <= n - 3 < NB:
                    u = n - 3
                    pe.wait_ge(sg["a_sb"], u + 1)
                    for k in range(2):
                        mm = pe.transpose(bank[4 + k][0:HD, 384:512], am[:, u % 2, k * HD:k * HD + HD], ident)
                    mm.then_inc(sg["aT_ps"], 1)
                if 0 <= n - 2 < NU:
                    u = n - 2
                    r = mrows(u // 2)
                    pe.wait_ge(sg["p1_norm"], u + 1)
                    for x in range(HH):
                        mm = pe.transpose(bank[4 + x // 3][0:M, (x % 3) * 128:(x % 3) * 128 + r],
                                          P1[0:r, u % 3, x * M:x * M + M], ident[0:r, 0:r])
                    mm.then_inc(sg["p1T_ps"], 1)
                if 0 <= n - 2 < NB:
                    u = n - 2
                    pe.wait_ge(sg["pT_sb"], u + 1)
                    pe.wait_ge(sg["v_mask"], u + 1)
                    if u >= 1:
                        pe.wait_ge(sg["a_sb"], u)
                    for g in range(4):
                        for e in range(2):
                            mm = pe.matmul(bank[7][64 * e:64 * e + 64, g * 48:g * 48 + 48], PT[0:TILE, u % 2, g, 64 * e:64 * e + 64],
                                           Vb[0:TILE, 2 * u + e, g * 48:g * 48 + 48], start=True, stop=True)
                    mm.then_inc(sg["av_ps"], 1)
                if 0 <= n - 1 < NB:
                    u = n - 1
                    pe.wait_ge(sg["p_exp"], u + 1)
                    if u >= 1:
                        pe.wait_ge(sg["pT_sb"], u)
                    for g in range(4):
                        mm = pe.transpose(bank[1][0:TILE, g * 128:g * 128 + 128], Ps[:, u % 2, g * TILE:g * TILE + TILE], ident)
                    mm.then_inc(sg["pT_ps"], 1)
                if n == NU:
                    pe.wait_ge(ld_late, 80)
                    pe.wait_ge(filled, 10)
                    pe.wait_ge(sg["p_sub"], NB)
                    pe.wait_ge(sg["pT_sb"], NB)
                if n in (NU, NU + 1):
                    m = n - NU
                    alpha(0, m, m, 0).then_inc(sg["al_ps"], 1)
            pe.wait_ge(sg["aT_sb"], NB)
            pe.wait_ge(sg["p1_exp"], 2 * NU)
            for m in range(2):
                alpha(1, m, 2 + m, 0).then_inc(sg["al_ps"], 1)
            pe.wait_ge(sg["a_sb"], NB)
            pe.wait_ge(sg["fT_sb"], 1)
            project(0)
            project(1)
            pe.wait_ge(sg["a1T_sb"], NU)
            alpha(2, 0, 1, 0)
            alpha(2, 1, 1, 256).then_inc(sg["al_ps"], 1)

            def hn_transpose(i):
                pe.wait_ge(sg["hn_sb"], i + 1)
                if i >= 2:
                    pe.wait_ge(sg["hnT_sb"], i - 1)
                for k in range(2):
                    mm = pe.transpose(bank[i % 2][0:HD, k * TILE:k * TILE + TILE], hn[0:TILE, i, k * HD:k * HD + HD],
                                      ident[0:TILE, 0:TILE])
                mm.then_inc(sg["hnT_ps"], 1)

            def products(i):
                pe.wait_ge(sg["hnT_sb"], i + 1)
                for k in range(2):
                    mm = pe.matmul(bank[2][0:TILE, i * S:i * S + S], hnT[0:HD, k, i * TILE:i * TILE + TILE], slT[0:HD, k, :],
                                   start=(k == 0), stop=(k == 1))
                return mm

            pe.wait_ge(sg["fT_sb"], 2)
            project(2)
            project(3)
            pe.wait_ge(sg["hn_sb"], 2)
            hn_transpose(0)
            pe.wait_ge(sg["fT_sb"], 3)
            project(4)
            project(5)
            hn_transpose(1)
            for i in range(2, NT):
                hn_transpose(i)
                products(i - 2)
            products(NT - 2)
            products(NT - 1).then_inc(sg["G_ps"], 1)
            pe.wait_ge(sg["L_sb"], 1)
            for i in range(NT):
                mm = pe.transpose(bank[3 + i // 3][0:S, (i % 3) * TILE:(i % 3) * TILE + TILE], L[0:TILE, i, :], ident[0:TILE, 0:TILE])
                if i % 3 == 2:
                    mm.then_inc(sg["LT_ps"], 1)
            pe.wait_ge(sg["LT_nrm"], 1)
            pe.wait_ge(filled, 12)
            for i in range(NT):
                mm = pe.transpose(bank[5 - i // 3][0:TILE, (i % 3) * S:(i % 3) * S + S], LTe[0:S, i * TILE:i * TILE + TILE], ident[0:S, 0:S])
                if i % 3 == 2:
                    mm.then_inc(sg["D_ps"], 1)
            for i in range(NT):
                m = imgs_of(i)
                pe.wait_ge(sg["D_sb"], i // 3 + 1)
                if i >= 2:
                    pe.wait_ge(sg["yA_sb"], i - 1)
                    pe.wait_ge(sg["yB_sb"], 2 * (i - 1))
                pe.matmul(bank[6 + i % 2][:, 0:m * S], hn[0:TILE, i, 0:128], Dm[0:TILE, i, 0:m, :], start=True, stop=True)
                for e in range(2):
                    mm = pe.matmul(bank[i % 2][64 * e:64 * e + 64, 0:m * S // 2], hn[0:TILE, i, 128:D], Dm[0:TILE, i, 0:m, e::2],
                                   start=True, stop=True)
                mm.then_inc(sg["y_ps"], 1)

            def fc1(n, q, r, u, rounds, first=False):
                if q == 0:
                    pe.wait_ge(sg["ys_sb"], n + 1)
                    pe.wait_ge(ld_b1[r], 16 * rounds)
                    pe.wait_ge(ld_w1[r], 48 * rounds)
                if not first:
                    pe.wait_ge(sg["gelu_sb"], 2 * n + (q - 1))
                cols = slice(q * 384, q * 384 + 384)
                pe.matmul(bank[q][:, 0:384], ind4[r], b1g[r][:, cols], start=True, stop=False, skip_group_check=True)
                for k in range(2):
                    for j in range(GS):
                        w = w1a(r)[:, j, cols] if k == 0 else w1b(r)[:, j // 2, cols]
                        mm = pe.matmul(bank[q][32 * j:32 * j + 32, 0:384], ys[:, u, k, j, :], w, start=False,
                                       stop=(k == 1), skip_group_check=True)
                mm.then_inc(sg["g1_ps"], 1)

            def turn(n, u):
                pe.wait_ge(sg["gelu_sb"], 2 * n + 2)
                for c in range(6):
                    mm = pe.transpose(bank[2 + c // 3][:, (c % 3) * 128:(c % 3) * 128 + 128], hg[:, u, c::6], ident)
                    if c % 3 == 2:
                        mm.then_inc(sg["hT_ps"], 1)

            def fc2(n, r, u, rounds, first=False):
                pe.wait_ge(ld_w2[r], 16 * rounds)
                if not first:
                    pe.wait_ge(sg["y2_sb"], n - 1)
                for c in range(6):
                    if c % 3 == 0:
                        pe.wait_ge(sg["hT_sb"], 2 * n + (c // 3 + 1))
                    for j in range(GS):
                        mm = pe.matmul(bank[4 + u][32 * j:32 * j + 32, 0:D], hT[:, u, c, 32 * j:32 * j + 32], w2r(r)[:, j, c, :],
                                       start=(c == 0), stop=(c == 5))
                mm.then_inc(sg["y2_ps"], 1)

            fc1(0, 0, 0, 0, 1, first=True)
            fc1(0, 1, 0, 0, 1, first=True)
            def combine_weights():
                pe.wait_ge(sg["Lc_nrm"], 1)
                pe.wait_ge(sg["yA_sb"], NT)
                pe.wait_ge(sg["yB_sb"], 2 * NT)
                for i in range(NT):
                    mm = pe.transpose(bank[6 + i // 3][0:S, (i % 3) * TILE:(i % 3) * TILE + TILE], Le[0:TILE, i, :], ident[0:TILE, 0:TILE])
                    if i % 3 == 2:
                        mm.then_inc(sg["C_ps"], 1)
                pe.wait_ge(sg["C_sb"], 2)
                for i in range(NT):
                    r = rows_of(i)
                    if i >= 2:
                        pe.wait_ge(sg["h1b_sb"], i - 1)
                    pe.matmul(bank[6 + i % 2][0:r, 0:D], C[0:S, i * TILE:i * TILE + r], b2s[0:S, :], start=True, stop=True)\
                        .then_inc(sg["cb_ps"], 1)

            def step(n, r, i, first=False):
                q = r + 1
                rounds = i + (q // RING + 1)
                fc1(n, 0, q % RING, q % 2, rounds)
                turn(n - 1, r % 2)
                fc1(n, 1, q % RING, q % 2, rounds)
                fc2(n - 1, r, r % 2, i + 1, first=first)

            for r in range(RING):
                step(r + 1, r, 0, first=(r < 2))
                if r == 0:
                    combine_weights()
            with pe.Fori(1, NG // RING - 1) as i:
                for r in range(RING):
                    step(i * RING + (r + 1), r, i)
            i = NG // RING - 1
            for r in range(RING - 1):
                step(i * RING + r + 1, r, i)
            turn(NG - 1, (NG - 1) % 2)
            fc2(NG - 1, RING - 1, (NG - 1) % 2, NG // RING)

            for u in range(RING):
                pe.wait_ge(y_ld[u], 64 * (NG // RING - (u == RING - 1)))
            pe.wait_ge(y_last, 64)
            for q in range(4):
                for x in range(2):
                    for e in range(2):
                        b = 4 * q + 2 * x + e
                        mm = pe.matmul(bank[q][64 * e:64 * e + T, x * D:x * D + D], C[0:S, b * T:b * T + T], Y[0:S, b, :],
                                       start=True, stop=True)
                mm.then_inc(sg["o_ps"], 1)


_ORDER = ["xT", "wT", "cst", "L0_tok_b", "L0_attn_w_attn", "L0_attn_b_attn", "L0_attn_w_proj", "L0_attn_b_proj",
          "L0_attn_w_mem", "L0_attn_b_mem", "L0_attn_w_alpha", "L0_attn_b_alpha", "memT", "L0_ffn_slots",
          "L0_ffn_scale", "L0_ffn_fc1_weight", "L0_ffn_fc1_bias", "L0_ffn_fc2_weight", "L0_ffn_fc2_bias",
          "L0_ffn_norm_weight"]


def constants():
    n = np.arange(8)
    dct = np.sqrt(2.0 / 8) * np.cos(np.pi * (2 * n[None, :] + 1) * n[:, None] / 16)
    dct[0] /= np.sqrt(2.0)
    p = np.arange(128)
    c = np.zeros((128, NCST), np.float32)
    c[:, C_ID:C_ID + 128] = np.eye(128)
    c[:, C_G:C_G + 128] = np.kron(dct, np.kron(np.eye(2), dct))
    for o in (0, 64):
        c[o:o + GS, C_IND:C_IND + 128] = p[None, :] // 32 == np.arange(GS)[:, None]
    c[:, C_MK:C_MK + HH] = p[:, None] // DH == np.arange(HH)[None, :]
    c[:, C_MV:C_MV + 3] = p[:, None] // T == np.arange(3)[None, :]
    return c


def kernel(**inputs):
    import concourse.bacc as bacc
    from concourse.bass_utils import run_bass_kernel_spmd

    a = {k: np.asarray(v) for k, v in inputs.items()}
    a["xT"] = a["x"].reshape(B, 3, 6, 2, 8, 6, 16).transpose(4, 6, 1, 3, 0, 2, 5).reshape(128, 6 * NTOK)
    a["wT"] = a["L0_tok_w"].reshape(D, 3, 2, 8, 16).transpose(3, 4, 1, 2, 0).reshape(128, 6 * D)
    a["memT"] = a["L0_attn_memory_features"][0].T
    a["cst"] = constants()
    nc = bacc.Bacc("TRN2", target_bir_lowering=False, num_devices=1)
    arrays, args = {}, []
    for name in _ORDER:
        v = np.ascontiguousarray(a[name])
        arrays[f"in_{name}"] = v
        args.append(nc.dram_tensor(f"in_{name}", v.shape, mybir.dt.from_np(v.dtype), kind="ExternalInput").ap())
    args.append(nc.dram_tensor("out_0", (B, T, D), F32, kind="ExternalOutput").ap())
    vit_tower(nc, *args)
    return run_bass_kernel_spmd(nc, [arrays], core_ids=[0]).results[0]["out_0"]
```

```python
from contextlib import ExitStack

import numpy as np

import concourse.bass as bass
from concourse import mybir

F32 = mybir.dt.float32
ALU = mybir.AluOpType
ACT = mybir.ActivationFunctionType
AX = mybir.AxisListType

B, T, D = 16, 36, 192
NTOK = B * T
TILE = 3 * T
NT = 6
PADTOK = NT * TILE
H, DH, M = 12, 16, 100
HD = D // 2
HH = H // 2
S, F = 64, 768
GS = 4
NG = S // GS
RING = 4
BP = 32
EPS = 1e-5

C_ID, C_G, C_IND, C_MK, C_MV, C_MB, NCST = 0, 128, 256, 384, 390, 393, 409


def rows_of(i):
    return TILE if i < NT - 1 else NTOK - TILE * (NT - 1)


def mrows(i):
    return min(128, NTOK - 128 * i)


def imgs_of(i):
    return rows_of(i) // T


def vit_tower(nc, xT_d, wT_d, cst_d, tok_b, w_attn, b_attn, w_proj, b_proj, w_mem, b_mem, w_alpha, b_alpha,
              memT_d, slots, scale, w1, b1, w2, b2, norm_w, out):
    with ExitStack() as ctx:
        def sb(name, n):
            return ctx.enter_context(nc.sbuf_tensor(name, [128, n], F32))

        def sem(name):
            return ctx.enter_context(nc.semaphore(name))

        GW = GS * F + (GS // 2) * F + GS * (F // 128) * D
        ring = sb("ring", RING * GW)
        front = sb("front", 11648)
        h = sb("h", NT * D)[:, :].rearrange("p (i d) -> p i d", i=NT)
        cst = sb("cst", NCST)
        tokb = sb("tokb", D)
        normb = sb("normb", D)
        a1buf = sb("a1buf", 2 * NTOK)
        a1T = a1buf[:, :].rearrange("p (k t) -> p k t", k=2)
        Vs = a1buf[:, :].rearrange("p (i d) -> p i d", i=NT)
        y2 = a1buf[:, 0:RING * D].rearrange("p (u n) -> p u n", u=RING)
        C = sb("C", PADTOK)
        stats = sb("stats", NT * 8)[:, :].rearrange("p (i c) -> p i c", i=NT)
        small = sb("small", 290)

        def w1a(r):
            return ring[:, r * GW:r * GW + GS * F].rearrange("p (s n) -> p s n", s=GS)

        def w1b(r):
            o = r * GW + GS * F
            return ring[:, o:o + GS // 2 * F].rearrange("p (s n) -> p s n", s=GS // 2)

        def w2r(r):
            o = r * GW + GS * F + GS // 2 * F
            return ring[:, o:(r + 1) * GW].rearrange("p (s c n) -> p s c n", s=GS, c=F // 128)

        def late(o, n):
            o += (RING - 1) * GW
            return ring[:, o:o + n]

        xT = late(0, 3456).rearrange("p (c t) -> p c t", c=6)
        wT = late(3456, 1152)
        weff = late(4608, 1152).rearrange("p (c o) -> p c o", c=6)
        Vb = late(0, 3072).rearrange("p (b n) -> p b n", b=B)
        Kb = late(3072, 1728).rearrange("p (b k n) -> p b k n", b=4, k=2)
        P1 = late(4800, 1800).rearrange("p (u n) -> p u n", u=3)
        P1T = late(6600, 1536).rearrange("p (u h t) -> p u h t", u=2, h=HH)
        Ps = late(8136, 864).rearrange("p (u n) -> p u n", u=2)

        def fr(o, n):
            return front[:, o:o + n]

        wA = fr(0, 1152).rearrange("p (k n) -> p k n", k=2)
        wM = fr(1152, 768).rearrange("p (k n) -> p k n", k=2)
        xlT = fr(1920, 1296).rearrange("p (k t) -> p k t", k=2)
        qT = fr(3216, 1216).rearrange("p (k t) -> p k t", k=2)
        kT = fr(4432, 1152).rearrange("p (k t) -> p k t", k=2)
        wAl = fr(5584, 768).rearrange("p (k n) -> p k n", k=4)
        wP = fr(6352, 384).rearrange("p (k n) -> p k n", k=2)
        memT = fr(6736, 200).rearrange("p (k n) -> p k n", k=2)
        PT = fr(6936, 1024).rearrange("p (u g n) -> p u g n", u=2, g=4)
        am = fr(7960, 384).rearrange("p (u n) -> p u n", u=2)
        aT = fr(8344, 1152).rearrange("p (k t) -> p k t", k=2)
        MKb = fr(9496, 1200).rearrange("p (k n) -> p k n", k=2)
        MVz = fr(10696, 384).rearrange("p (h n) -> p h n", h=H)
        th = fr(0, 1152).rearrange("p (k t) -> p k t", k=2)
        sm = fr(1152, 1152).rearrange("p (k t) -> p k t", k=2)
        df = fr(2304, 1152).rearrange("p (k t) -> p k t", k=2)
        fT = fr(3456, 1152).rearrange("p (k t) -> p k t", k=2)
        hn = fr(6736, 1152).rearrange("p (i d) -> p i d", i=NT)
        hnT = fr(9496, 1296).rearrange("p (k t) -> p k t", k=2)
        L = fr(5584, 384).rearrange("p (i s) -> p i s", i=NT)
        Le = fr(5968, 384).rearrange("p (i s) -> p i s", i=NT)
        LTe = fr(7888, 648)
        Dm = fr(8960, 1152).rearrange("p (i b s) -> p i b s", i=NT, b=3)
        yA = fr(10112, 1024).rearrange("p (s b) -> p s b", s=S)
        yB = fr(11136, 512).rearrange("p (s b) -> p s b", s=S // 2)
        hg = fr(0, 1536).rearrange("p (u n) -> p u n", u=2)
        hT = fr(1536, 1536).rearrange("p (u c m) -> p u c m", u=2, c=6)
        b1f = fr(3072, 1536).rearrange("p (u n) -> p u n", u=2)
        ys = fr(4608, 512).rearrange("p (u w j b) -> p u w j b", u=2, w=2, j=GS)
        Cc = fr(5504, NG * T).rearrange("p (g t) -> p g t", g=NG)
        Cbd = fr(6080, 2 * NTOK).rearrange("p (u n) -> p u n", u=2)

        xl = sb("xl", 2 * D)[:, :].rearrange("p (u d) -> p u d", u=2)
        bnst, epsc, b2s = sb("bnst", 12), sb("epsc", 1), sb("b2s", D)
        slr, squares = fr(11080, D), fr(11272, D)
        slT = fr(11464, 2 * S).rearrange("p (k s) -> p k s", k=2)

        ident = cst[:, C_ID:C_ID + 128]
        dct = cst[:, C_G:C_G + 128]
        b1g = [b1f[64 * (r // 2):64 * (r // 2) + GS, r % 2, :] for r in range(RING)]
        ind4 = [cst[64 * (r // 2):64 * (r // 2) + GS, C_IND:C_IND + 128] for r in range(RING)]
        mask_k = cst[0:HD, C_MK:C_MK + HH]
        mask_v = cst[0:TILE, C_MV:C_MV + 3]
        mask_b = cst[:, C_MB:C_MB + B]

        bank = [ctx.enter_context(nc.psum_tensor(f"bank{i}", [128, 512], F32)) for i in range(8)]

        ld_cst, ld_wT, ld_x0, ld_x1, ld_mem, ld_attn, ld_rows, ld_late = (sem("ld_" + n) for n in (
            "cst", "wT", "x0", "x1", "mem", "attn", "rows", "late"))
        ld_w1 = [sem(f"ld_w1_{r}") for r in range(RING)]
        ld_w2 = [sem(f"ld_w2_{r}") for r in range(RING)]
        ld_b1 = [sem(f"ld_b1_{r}") for r in range(RING)]
        ld_w1_start = sem("ld_w1_start")
        ld_w2_end = sem("ld_w2_end")
        cc_ld = [sem(f"cc_ld_{u}") for u in range(RING)]
        filled = sem("filled")
        dve = sem("dve_chain")
        act = sem("act_chain")
        pool = sem("pool_chain")
        names = ("weff_ps weff_sb h_ps var_sb std_sb xl_sb xlT_ps xlT_sb qk_ps q_sb k_sb v_ps v_sb v_ld v_mask mk_ps mk_sb "
                 "mv_ps mv_sb sl_std sl_sb slT_ps slT_sb kb_sb s1_ps p1_max p1_exp p1_rec p1_norm p1T_ps p1T_sb "
                 "a1T_ps a1T_sb s_ps p_sub p_exp pT_ps pT_sb av_ps a_sb aT_ps aT_sb al_ps th_sb sumdif fT_sb pr_ps "
                 "hn_sb ss_sb hnT_ps hnT_sb G_ps veps std2 ms2 rms L_sb LT_ps LT_sub LT_exp LT_nrm Lc_sub Lc_exp Lc_nrm D_ps D_sb "
                 "y_ps yA_sb yB_sb C_ps C_sb cc_zero cbd_sb comb_ps "
                 "ys_sb g1_ps gelu_sb hT_ps hT_sb y2_ps y2_sb o_ps o_sb o1_sb stored").split()
        sg = {n: sem(n) for n in names}

        PRB = (7, 0, 4, 5, 6, 7)
        X = small[:, 0:84]
        smask = small[:, 90:108].rearrange("p (i b) -> p i b", i=NT)

        def total(i):
            return bank[5 + i // 2][0:rows_of(i), (i % 2) * D:(i % 2) * D + D]

        block = ctx.enter_context(nc.Block())
        NB = B // 2
        NM = -(-NTOK // 128)
        NU = 2 * NM
        STEPS = NU + 3
        NHALF = NTOK // 2
        CHUNKS = ((0, NHALF), (NHALF, 512), (512, NTOK))
        CHUNK_PAIRS = (NB // 2, NB, NB)
        CHUNK_UNITS = (6, 8, NU)

        @block.sync
        def _(sp):
            sp.dma_start(cst[:, :], cst_d).then_inc(ld_cst, 16)
            sp.dma_start(wT, wT_d).then_inc(ld_wT, 16)
            xv = xT_d.rearrange("p (c t) -> p c t", c=6)
            sp.dma_start(xT[:, :, 0:3 * TILE], xv[:, :, 0:3 * TILE]).then_inc(ld_x0, 16)
            sp.dma_start(xT[:, :, 3 * TILE:NTOK], xv[:, :, 3 * TILE:NTOK]).then_inc(ld_x1, 16)

            def load_w1(g, r):
                sp.dma_start(w1a(r), w1[bass.ds(g * GS, GS), 0:128, :].rearrange("s p n -> p s n")).then_inc(ld_w1[r], 16)
                v = w1[bass.ds(g * GS, GS), 128:D, :].rearrange("(q e) p n -> e p q n", e=2)
                for e in range(2):
                    sp.dma_start(w1b(r)[64 * e:64 * e + 64], v[e]).then_inc(ld_w1[r], 16)

            def load_w2(g, r):
                sp.dma_start(w2r(r), w2[bass.ds(g * GS, GS), :, :].rearrange("s (p c) n -> p s c n", c=6)).then_inc(ld_w2[r], 16)

            sp.wait_ge(ld_late, 80)
            for r in range(2):
                load_w1(r, r)
                load_w2(r, r)
            sp.wait_ge(sg["v_sb"], NT)
            for r in range(3):
                for b in range(3):
                    m = NT - (b > 0)
                    sp.dma_start(Vb[T * r:T * r + T, b:b + 3 * (m - 1) + 1:3, :], Vs[T * b:T * b + T, 0:m, :]).then_inc(sg["v_ld"], 16)
            load_w1(2, 2)
            load_w2(2, 2)
            sp.wait_ge(sg["av_ps"], NB)
            load_w1(3, 3)
            sp.wait_ge(sg["a1T_sb"], NU)
            load_w2(3, 3)
            for x in range(2):
                sp.wait_ge(sg["g1_ps"], x + 1)
                c = slice(384 * x, 384 * x + 384)
                ld = (ld_w1_start, ld_w1[0])[x]
                sp.dma_start(w1a(0)[:, :, c], w1[RING * GS:(RING + 1) * GS, 0:128, c].rearrange("s p n -> p s n")).then_inc(ld, 16)
                v = w1[RING * GS:(RING + 1) * GS, 128:D, c].rearrange("(q e) p n -> e p q n", e=2)
                for e in range(2):
                    sp.dma_start(w1b(0)[64 * e:64 * e + 64, :, c], v[e]).then_inc(ld, 16)
            with sp.Fori(1, NG // RING - 1) as i:
                for r in range(RING):
                    q = r + 1
                    sp.wait_ge(sg["g1_ps"], (i - 1) * (2 * RING) + (2 * q + 2))
                    load_w1(i * RING + q, q % RING)
                    sp.wait_ge(sg["y2_ps"], (i - 1) * RING + (r + 1))
                    load_w2(i * RING + r, r)
            for r in range(RING):
                g = NG - RING + r
                if r < RING - 1:
                    sp.wait_ge(sg["g1_ps"], 2 * (g + 1 - RING) + 2)
                    load_w1(g + 1, r + 1)
                sp.wait_ge(sg["y2_ps"], g - RING + 1)
                if r < RING - 1:
                    load_w2(g, r)
            v = w2[NG * GS - GS:NG * GS, :, :].rearrange("s (p c) n -> p s c n", c=6)
            for x in range(2):
                c = slice(3 * x, 3 * x + 3)
                sp.dma_start(w2r(RING - 1)[:, :, c, :], v[:, :, c, :]).then_inc((ld_w2[RING - 1], ld_w2_end)[x], 16)

            ov = out.rearrange("b t d -> (b t) d")
            for q in range(2):
                sp.wait_ge(sg[("o_sb", "o1_sb")[q]], 1)
                sp.dma_start(ov[2 * q * TILE:2 * (q + 1) * TILE, :].rearrange("(i p) d -> p i d", i=2), h[0:TILE, 2 * q:2 * q + 2, :])\
                    .then_inc(sg["stored"], 16)
            sp.wait_ge(sg["o_sb"], 2)
            for i in (4, 5):
                sp.dma_start(ov[i * TILE:i * TILE + rows_of(i), :], h[0:rows_of(i), i, :]).then_inc(sg["stored"], 16)
            sp.wait_ge(sg["stored"], 4 * 16)

        @block.gpsimd
        def _(gp):
            ended = {}

            def alone(ins, ready=pool):
                ended[ready.name] = ended.get(ready.name, 0) + 1
                ins.then_inc(ready, 1)
                gp.wait_ge(ready, ended[ready.name])

            alone(gp.memset(memT[96:97, 1, :], 1.0), filled)
            alone(gp.memset(epsc[:, :], EPS), filled)
            alone(gp.memset(MVz[:, :, :], 0.0), filled)
            alone(gp.memset(h[:, NT - 1, :], 0.0), filled)
            alone(gp.memset(xlT[96:97, :, :], 1.0), filled)
            alone(gp.memset(qT[:, :, NTOK:608], 0.0), filled)
            alone(gp.memset(qT[96:128, :, 0:NTOK], 0.0), filled)
            alone(gp.memset(MKb[96:128, :, :], 0.0), filled)
            alone(gp.memset(P1T[96:128, :, :, :], 0.0), filled)
            alone(gp.memset(aT[96:97, 1, :], 1.0), filled)

            def k_blocks(i):
                if i >= 2:
                    gp.wait_ge(sg["s_ps"], i - 1)
                for k in range(2):
                    b = 2 * i
                    alone(gp.tensor_tensor(
                        Kb[0:HD, b % 4:b % 4 + 2, k, :].rearrange("p e (h t) -> p e h t", h=HH),
                        kT[0:HD, k, b * T:b * T + 2 * T].rearrange("p (e t) -> p e t", e=2).unsqueeze(2).broadcast_to([HD, 2, HH, T]),
                        mask_k.unsqueeze(1).unsqueeze(3).broadcast_to([HD, 2, HH, T]), ALU.mult), sg["kb_sb"] if k == 1 else pool)

            def sum_and_difference(n):
                gp.wait_ge(sg["aT_sb"], CHUNK_PAIRS[n])
                gp.wait_ge(sg["a1T_sb"], CHUNK_UNITS[n])
                c = slice(*CHUNKS[n])
                alone(gp.tensor_tensor(df[0:HD, :, c], aT[0:HD, :, c], a1T[0:HD, :, c], ALU.subtract), sg["sumdif"])
                alone(gp.tensor_tensor(sm[0:HD, :, c], aT[0:HD, :, c], a1T[0:HD, :, c], ALU.add), sg["sumdif"])

            gp.wait_ge(ld_cst, 16)
            gp.wait_ge(sg["k_sb"], 2)
            k_blocks(0)
            k_blocks(1)
            for n in range(NU):
                if n + 2 == NB // 2:
                    gp.wait_ge(sg["k_sb"], 4)
                if n + 2 < NB:
                    k_blocks(n + 2)
                if n == NU - 1:
                    gp.wait_ge(sg["s_ps"], NB)
                    sum_and_difference(0)
                r = mrows(n // 2)
                gp.wait_ge(sg["p1_rec"], n + 1)
                v = P1[0:r, n % 3, :].rearrange("p (h m) -> p h m", h=HH)
                alone(gp.tensor_tensor(v, v, small[0:r, 24 * (n % 3) + 12:24 * (n % 3) + 18].unsqueeze(2).broadcast_to([r, HH, M]),
                                       ALU.mult), sg["p1_norm"])

            gp.wait_ge(sg["s1_ps"], 2 * NU)
            alone(gp.memset(fT[96:97, 1, :], 2.0), filled)
            sum_and_difference(1)
            sum_and_difference(2)
            gp.wait_ge(sg["al_ps"], 5)
            alone(gp.memset(LTe[0:S, NTOK:PADTOK], 0.0), filled)

            gp.wait_ge(sg["C_ps"], 2)
            alone(gp.memset(Cc[:, :, :], 0.0), sg["cc_zero"])
            gp.wait_ge(sg["C_sb"], 2)

            def move(g):
                if g >= RING:
                    gp.wait_ge(cc_ld[g % RING], 64 * (g // RING))
                for j in range(GS):
                    slot = g * GS + j
                    gp.dma_start(Cc[BP * j:BP * j + B, g, :], C[slot:slot + 1, 0:NTOK].rearrange("p (b t) -> p b t", b=B))\
                        .then_inc(cc_ld[g % RING], 16)

            move(0)
            move(1)
            for g in range(NG):
                for x in (2 * g + 2, 2 * g + 3):
                    if x < NG:
                        move(x)
                gp.wait_ge(cc_ld[g % RING], 64 * (g // RING + 1))
                if g >= 2:
                    gp.wait_ge(sg["comb_ps"], g - 1)
                alone(gp.tensor_tensor(Cbd[:, g % 2, :].rearrange("p (b t) -> p b t", b=B),
                                       Cc[:, g, :].unsqueeze(1).broadcast_to([128, B, T]),
                                       mask_b.unsqueeze(2).broadcast_to([128, B, T]), ALU.mult), sg["cbd_sb"])

        @block.scalar
        def _(sc):
            half = "(k p) n -> p k n"
            sc.dma_start(memT[0:HD], memT_d.rearrange(half, k=2)).then_inc(ld_mem, 16)
            sc.dma_start(wM[0:HD], w_mem.rearrange(half, k=2)).then_inc(ld_mem, 16)
            sc.dma_start(wM[96:97, 1, :], b_mem.unsqueeze(0)).then_inc(ld_mem, 16)
            sc.dma_start(tokb[:, :], tok_b.unsqueeze(0).broadcast_to([128, D])).then_inc(ld_rows, 16)
            sc.dma_start(normb[:, :], norm_w.unsqueeze(0).broadcast_to([128, D])).then_inc(ld_rows, 16)
            sc.dma_start(slr[0:S, :], slots).then_inc(ld_rows, 16)
            sc.dma_start(small[0:S, 289:290], scale.unsqueeze(1)).then_inc(ld_rows, 16)
            sc.dma_start(wA[0:HD], w_attn.rearrange(half, k=2)).then_inc(ld_attn, 16)
            sc.dma_start(wA[96:97, 1, :], b_attn.unsqueeze(0)).then_inc(ld_attn, 16)
            sc.dma_start(wAl[0:HD], w_alpha.rearrange("(k p) n -> p k n", k=4)).then_inc(ld_late, 16)
            sc.dma_start(wAl[96:97, 1, :], b_alpha.unsqueeze(0)).then_inc(ld_late, 16)
            sc.dma_start(wP[0:HD], w_proj.rearrange(half, k=2)).then_inc(ld_late, 16)
            sc.dma_start(wP[96:97, 1, :], b_proj.unsqueeze(0)).then_inc(ld_late, 16)
            sc.dma_start(b2s[0:S, :], b2).then_inc(ld_late, 16)

            def xlT_copy(i):
                sc.wait_ge(sg["xlT_ps"], i + 1)
                n = rows_of(i)
                sc.activation(xlT[0:HD, :, i * TILE:i * TILE + n],
                              bank[1 + i % 2][0:HD, 0:2 * TILE].rearrange("p (k t) -> p k t", k=2)[:, :, 0:n], ACT.Copy)\
                    .then_inc(sg["xlT_sb"], 1)

            sc.wait_ge(ld_rows, 64)
            sc.activation(squares[0:S, :], slr[0:S, :], ACT.Square, accum_out=small[0:S, 280:281]).then_inc(act, 1)
            sc.wait_ge(act, 1)
            sc.activation(small[0:S, 281:282], small[0:S, 280:281], ACT.Sqrt).then_inc(sg["sl_std"], 1)
            for i in range(NT):
                sc.wait_ge(sg["var_sb"], i + 1)
                sc.activation(stats[0:TILE, i, 3:4], stats[0:TILE, i, 2:3], ACT.Sqrt).then_inc(sg["std_sb"], 1)
                if i >= 1:
                    xlT_copy(i - 1)
            xlT_copy(NT - 1)
            sc.activation(small[0:S, 284:285], small[0:S, 280:281], ACT.Exp, scale=0.0)
            for u in range(4):
                n, m = divmod(u, 2)
                sc.wait_ge(sg["qk_ps"], 4 * n + m + 3)
                sc.activation(qT[0:HD, m, n * NHALF:(n + 1) * NHALF], bank[((5, 7), (5, 6))[n][m]][0:HD, 0:NHALF], ACT.Copy)\
                    .then_inc(sg["q_sb"], 1)

            def tanh(n, m):
                sc.wait_ge(sg["al_ps"], 2 * n + m + 1)
                c = slice(*CHUNKS[n])
                sc.activation(th[0:HD, m, c], bank[2 * n + m][0:HD, 0:c.stop - c.start], ACT.Tanh, scale=0.5).then_inc(sg["th_sb"], 1)

            def tanh_last():
                sc.wait_ge(sg["al_ps"], 5)
                c = slice(*CHUNKS[2])
                sc.activation(th[0:HD, :, c], bank[1][0:HD, :].rearrange("p (k t) -> p k t", k=2)[:, :, 0:c.stop - c.start],
                              ACT.Tanh, scale=0.5).then_inc(sg["th_sb"], 1)

            def hnT_copy(i):
                sc.wait_ge(sg["hnT_ps"], i + 1)
                sc.activation(hnT[0:HD, :, i * TILE:(i + 1) * TILE],
                              bank[i % 2][0:HD, 0:2 * TILE].rearrange("p (k t) -> p k t", k=2), ACT.Copy).then_inc(sg["hnT_sb"], 1)

            sc.wait_ge(filled, 9)
            for n in range(STEPS):
                if 0 <= n - 2 < NB:
                    u = n - 2
                    sc.wait_ge(sg["pT_ps"], u + 1)
                    if u >= 2:
                        sc.wait_ge(sg["av_ps"], u - 1)
                    sc.activation(PT[0:TILE, u % 2, :, :], bank[1][0:TILE, :].rearrange("p (g m) -> p g m", g=4), ACT.Copy)\
                        .then_inc(sg["pT_sb"], 1)
                if n < NB:
                    sc.wait_ge(sg["p_sub"], n + 1)
                    sc.activation(Ps[:, n % 2, :], Ps[:, n % 2, :], ACT.Exp).then_inc(sg["p_exp"], 1)
                if n < NU:
                    r = mrows(n // 2)
                    o = 24 * (n % 3)
                    for x in range(HH):
                        if x % 3 == 0:
                            sc.wait_ge(sg["p1_max"], 2 * n + x // 3 + 1)
                        if x == 0 and n >= 3:
                            sc.wait_ge(sg["p1T_ps"], n - 2)
                        e = sc.activation(P1[0:r, n % 3, x * M:x * M + M], bank[2 + x // 3][0:r, (x % 3) * M:(x % 3) * M + M], ACT.Exp,
                                          bias=small[0:r, o + x:o + x + 1], accum_out=small[0:r, o + 6 + x:o + 7 + x])
                        if x % 3 == 2:
                            e.then_inc(sg["p1_exp"], 1)
                if 0 <= n - 3 < NU:
                    u = n - 3
                    i, k = divmod(u, 2)
                    r = mrows(i)
                    sc.wait_ge(sg["a1T_ps"], u + 1)
                    if u == 0:
                        sc.wait_ge(sg["v_ld"], 16 * 9)
                    sc.activation(a1T[0:HD, k, i * 128:i * 128 + r], bank[6][0:HD, 0:r], ACT.Copy).then_inc(sg["a1T_sb"], 1)
                if 0 <= n - 2 < NU:
                    u = n - 2
                    r = mrows(u // 2)
                    sc.wait_ge(sg["p1T_ps"], u + 1)
                    if u >= 2:
                        sc.wait_ge(sg["a1T_ps"], u - 1)
                    for q in range(2):
                        ins = sc.activation(P1T[0:M, u % 2, 3 * q:3 * q + 3, 0:r],
                                            bank[4 + q][0:M, 0:384].rearrange("p (h t) -> p h t", h=3)[:, :, 0:r], ACT.Copy)
                    ins.then_inc(sg["p1T_sb"], 1)
                if 0 <= n - 3 < NB:
                    u = n - 3
                    sc.wait_ge(sg["aT_ps"], u + 1)
                    for k in range(2):
                        ins = sc.activation(aT[0:HD, k, 2 * T * u:2 * T * (u + 1)].rearrange("p (e t) -> p e t", e=2),
                                            bank[4 + k][0:HD, 384:512].rearrange("p (e t) -> p e t", e=2)[:, :, 0:T], ACT.Copy)
                    ins.then_inc(sg["aT_sb"], 1)
                if n in (NU, NU + 1):
                    tanh(0, n - NU)
            tanh(1, 0)
            tanh(1, 1)
            tanh_last()

            for i in range(NT):
                if i == 2:
                    sc.activation(small[0:S, 285:286], small[0:S, 280:281], ACT.Sqrt, scale=0.0)
                sc.wait_ge(sg["hn_sb"], i + 1)
                if i >= 2:
                    sc.wait_ge(sg["ss_sb"], i - 1)
                sc.activation(xl[0:TILE, i % 2, :], hn[0:TILE, i, :], ACT.Square, accum_out=X[0:TILE, 6 + i:7 + i]).then_inc(sg["ss_sb"], 1)
                if i >= 1:
                    hnT_copy(i - 1)
            hnT_copy(NT - 1)
            sc.wait_ge(sg["veps"], 1)
            sc.wait_ge(sg["ss_sb"], NT)
            sc.activation(X[0:TILE, 12:24], X[0:TILE, 0:12], ACT.Sqrt).then_inc(sg["std2"], 1)
            sc.wait_ge(sg["ms2"], 1)
            sc.activation(X[0:TILE, 36:42], X[0:TILE, 30:36], ACT.Sqrt, bias=epsc[0:TILE, 0:1]).then_inc(sg["rms"], 1)

            def biases(g, r):
                sc.dma_start(b1g[r], b1[bass.ds(g * GS, GS), :]).then_inc(ld_b1[r], 16)

            for r in range(RING):
                biases(r, r)
            for q in range(2):
                sc.wait_ge(sg["LT_sub"], q + 1)
                c = slice(324 * q, (324, NTOK)[q])
                sc.activation(LTe[0:S, c], LTe[0:S, c], ACT.Exp).then_inc(sg["LT_exp"], 1)
            for i in range(NT):
                m = imgs_of(i)
                sc.wait_ge(sg["y_ps"], i + 1)
                for e in range(2):
                    p = slice(64 * e, 64 * e + 64)
                    sc.activation(yB[p, :, 3 * i:3 * i + m].rearrange("p s b -> p b s"),
                                  bank[i % 2][p, 0:m * S // 2].rearrange("p (b s) -> p b s", b=m), ACT.Copy)\
                        .then_inc(sg["yB_sb"], 1)

            sc.wait_ge(sg["Lc_sub"], 1)
            sc.activation(Le[0:TILE], Le[0:TILE], ACT.Exp).then_inc(sg["Lc_exp"], 1)

            def gelu(n, u):
                for q in range(2):
                    sc.wait_ge(sg["g1_ps"], n * 2 + q + 1)
                    sc.activation(hg[:, u, q * 384:q * 384 + 384], bank[q][:, 0:384], ACT.Gelu).then_inc(sg["gelu_sb"], 1)

            with sc.Fori(0, NG // RING - 1) as i:
                for r in range(RING):
                    gelu(i * RING + r, r % 2)
                    biases(i * RING + (r + RING), r)
            for r in range(RING):
                gelu((NG // RING - 1) * RING + r, r % 2)
            sc.wait_ge(sg["o_ps"], 2)
            sc.activation(h[0:TILE, 2:4, :], bank[6][0:TILE, 0:2 * D].rearrange("p (i d) -> p i d", i=2), ACT.Copy)\
                .then_inc(sg["o1_sb"], 1)

        @block.vector
        def _(ve):
            chain = [0]

            def link(ins):
                chain[0] += 1
                ins.then_inc(dve, 1)
                ve.wait_ge(dve, chain[0])

            for q in range(3):
                ve.wait_ge(sg["weff_ps"], q + 1)
                ve.tensor_copy(weff[:, 2 * q:2 * q + 2, :], bank[q][:, 0:384].rearrange("p (c o) -> p c o", c=2))\
                    .then_inc(sg["weff_sb"], 1)
            ve.wait_ge(ld_cst, 16)
            ve.wait_ge(sg["mk_ps"], 1)
            for k in range(2):
                ins = ve.tensor_tensor(MKb[0:HD, k, :].rearrange("p (h m) -> p h m", h=HH),
                                       bank[5][0:HD, k * M:k * M + M].unsqueeze(1).broadcast_to([HD, HH, M]),
                                       mask_k.unsqueeze(2).broadcast_to([HD, HH, M]), ALU.mult)
            ins.then_inc(sg["mk_sb"], 1)
            ve.wait_ge(sg["mv_ps"], 1)
            ve.wait_ge(filled, 3)
            for e in range(2):
                ins = ve.tensor_copy(MVz[0:M, e::2, DH * e:DH * e + DH],
                                     bank[6][0:M, 0:D].rearrange("p (h e c) -> p h e c", e=2, c=DH)[:, :, e, :])
            ins.then_inc(sg["mv_sb"], 1)
            ve.wait_ge(sg["sl_std"], 1)
            link(ve.tensor_scalar(small[0:S, 282:283], small[0:S, 281:282], EPS, None, ALU.max))
            link(ve.reciprocal(small[0:S, 283:284], small[0:S, 282:283]))
            ve.tensor_scalar(slr[0:S, :], slr[0:S, :], small[0:S, 283:284], small[0:S, 289:290], ALU.mult, ALU.mult)\
                .then_inc(sg["sl_sb"], 1)

            ve.wait_ge(filled, 4)
            for i in range(NT + 1):
                if i < NT:
                    r = rows_of(i)
                    ve.wait_ge(sg["h_ps"], i + 1)
                    link(ve.tensor_tensor(h[0:r, i, :], bank[(3 + i) % 8][0:r, 0:D], tokb[0:r, :], ALU.add))
                    link(ve.bn_stats(bnst[0:TILE, 0:6], h[0:TILE, i, :]))
                    link(ve.bn_aggr(stats[0:TILE, i, 0:2], bnst[0:TILE, 0:6]))
                    ve.tensor_scalar(stats[0:TILE, i, 2:3], stats[0:TILE, i, 1:2], EPS, None, ALU.add).then_inc(sg["var_sb"], 1)
                if i >= 1:
                    j = i - 1
                    ve.wait_ge(sg["std_sb"], i)
                    if i >= 3:
                        ve.wait_ge(sg["xlT_ps"], i - 2)
                    link(ve.reciprocal(stats[0:TILE, j, 4:5], stats[0:TILE, j, 3:4]))
                    ve.tensor_scalar(xl[0:TILE, j % 2, :], h[0:TILE, j, :], stats[0:TILE, j, 0:1], stats[0:TILE, j, 4:5],
                                     ALU.subtract, ALU.mult).then_inc(sg["xl_sb"], 1)
            ve.wait_ge(sg["slT_ps"], 1)
            ve.tensor_copy(slT[0:HD, :, :], bank[6][0:HD, 0:2 * S].rearrange("p (k s) -> p k s", k=2)).then_inc(sg["slT_sb"], 1)
            for u in range(4):
                n, m = divmod(u, 2)
                ve.wait_ge(sg["qk_ps"], 4 * n + m + 1)
                ve.tensor_copy(kT[0:HD, m, n * NHALF:(n + 1) * NHALF], bank[3 + m][0:HD, 0:NHALF]).then_inc(sg["k_sb"], 1)
            for i in range(NT):
                r = rows_of(i)
                ve.wait_ge(sg["v_ps"], i + 1)
                ve.tensor_copy(Vs[0:r, i, :], bank[7 - i % 2][0:r, 0:D]).then_inc(sg["v_sb"], 1)

            def fuse(n):
                c = slice(*CHUNKS[n])
                ve.wait_ge(sg["sumdif"], 2 * n + 2)
                ve.wait_ge(sg["th_sb"], (2, 4, 5)[n])
                ve.wait_ge(filled, 11)
                link(ve.tensor_tensor(df[0:HD, :, c], df[0:HD, :, c], th[0:HD, :, c], ALU.mult))
                ve.tensor_tensor(fT[0:HD, :, c], df[0:HD, :, c], sm[0:HD, :, c], ALU.add).then_inc(sg["fT_sb"], 1)

            def residual(i):
                def after(ins):
                    chain[0] += 1
                    ins.then_inc(dve, 1)
                    return chain[0]

                two = (i, i + 1)
                done = []
                for t in two:
                    r = rows_of(t)
                    ve.wait_ge(sg["pr_ps"], t + 1)
                    done.append(after(ve.scalar_tensor_tensor(out=h[0:r, t, :], in0=bank[PRB[t]][0:r, 0:D], scalar=0.5,
                                                              in1=h[0:r, t, :], op0=ALU.mult, op1=ALU.add)))
                for x, t in enumerate(two):
                    ve.wait_ge(dve, done[x])
                    done[x] = after(ve.bn_stats(bnst[0:TILE, 6 * x:6 * x + 6], h[0:TILE, t, :]))
                for x, t in enumerate(two):
                    ve.wait_ge(dve, done[x])
                    done[x] = after(ve.bn_aggr(stats[0:TILE, t, 0:2], bnst[0:TILE, 6 * x:6 * x + 6]))
                for x, t in enumerate(two):
                    ve.wait_ge(dve, done[x])
                    ve.scalar_tensor_tensor(out=hn[0:TILE, t, :], in0=h[0:TILE, t, :], scalar=stats[0:TILE, t, 0:1],
                                            in1=normb[0:TILE, :], op0=ALU.subtract, op1=ALU.mult).then_inc(sg["hn_sb"], 1)

            def minus_maxima(n, q):
                r = mrows(n // 2)
                ve.wait_ge(sg["s1_ps"], 2 * n + q + 1)
                ve.tensor_reduce(small[0:r, 24 * (n % 3) + 3 * q:24 * (n % 3) + 3 * q + 3],
                                 bank[2 + q][0:r, 0:300].rearrange("p (h m) -> p h m", h=3), AX.X, ALU.max, negate=True)\
                    .then_inc(sg["p1_max"], 1)

            for n in range(STEPS):
                if n < NB:
                    ve.wait_ge(sg["s_ps"], n + 1)
                    if n >= 2:
                        ve.wait_ge(sg["pT_ps"], n - 1)
                    sv = bank[0][:, 0:432].rearrange("p (h t) -> p h t", h=H)
                    mx = small[:, 140 + 36 * (n % 3):152 + 36 * (n % 3)]
                    link(ve.tensor_reduce(mx, sv, AX.X, ALU.max))
                    ve.tensor_tensor(Ps[:, n % 2, :].rearrange("p (h t) -> p h t", h=H), sv,
                                     mx.unsqueeze(2).broadcast_to([128, H, T]), ALU.subtract).then_inc(sg["p_sub"], 1)
                if n < NU:
                    minus_maxima(n, 0)
                if 0 <= n - 1 < NU:
                    r = mrows((n - 1) // 2)
                    o = 24 * ((n - 1) % 3)
                    ve.wait_ge(sg["p1_exp"], 2 * n)
                    ve.reciprocal(small[0:r, o + 12:o + 18], small[0:r, o + 6:o + 12]).then_inc(sg["p1_rec"], 1)
                if 0 <= n - 3 < NB:
                    u = n - 3
                    o = 140 + 36 * (u % 3) + 24
                    ve.wait_ge(sg["av_ps"], u + 1)
                    if u >= 2:
                        ve.wait_ge(sg["aT_ps"], u - 1)
                    ve.tensor_tensor(am[:, u % 2, :].rearrange("p (h c) -> p h c", h=H),
                                     bank[7][:, 0:D].rearrange("p (h c) -> p h c", h=H),
                                     small[:, o:o + H].unsqueeze(2).broadcast_to([128, H, DH]), ALU.mult).then_inc(sg["a_sb"], 1)
                if n < NU:
                    minus_maxima(n, 1)
                if 0 <= n - 2 < NB:
                    u = n - 2
                    if u == 0:
                        ve.wait_ge(sg["v_ld"], 16 * 9)
                    v = Vb[0:TILE, 2 * u:2 * u + 2, :].rearrange("p b (g r c) -> p (b g) r c", g=4, r=3)
                    ve.tensor_tensor(v, v, mask_v.unsqueeze(1).unsqueeze(3).broadcast_to([TILE, 8, 3, DH]), ALU.mult)\
                        .then_inc(sg["v_mask"], 1)
                if n < NB:
                    o = 140 + 36 * (n % 3)
                    ve.wait_ge(sg["p_exp"], n + 1)
                    link(ve.tensor_reduce(small[:, o + 12:o + 24], Ps[:, n % 2, :].rearrange("p (h t) -> p h t", h=H), AX.X, ALU.add))
                    link(ve.reciprocal(small[:, o + 24:o + 36], small[:, o + 12:o + 24]))
                if n == NU + 1:
                    fuse(0)
            fuse(1)
            residual(0)
            fuse(2)
            residual(2)
            residual(4)

            link(ve.tensor_copy(X[0:TILE, 24:30], stats[0:TILE, :, 1]))
            ve.tensor_scalar(X[0:TILE, 0:6], X[0:TILE, 24:30], EPS, None, ALU.add).then_inc(sg["veps"], 1)
            ve.wait_ge(sg["veps"], 1)
            link(ve.reciprocal(X[0:TILE, 42:48], X[0:TILE, 0:6]))
            ve.tensor_tensor(X[0:TILE, 30:36], X[0:TILE, 42:48], X[0:TILE, 24:30], ALU.mult).then_inc(sg["ms2"], 1)
            ve.wait_ge(sg["std2"], 1)
            ve.wait_ge(sg["rms"], 1)
            link(ve.tensor_tensor(X[0:TILE, 54:60], X[0:TILE, 36:42], X[0:TILE, 12:18], ALU.mult))
            link(ve.scalar_tensor_tensor(out=X[0:TILE, 66:72], in0=X[0:TILE, 54:60], scalar=EPS, in1=X[0:TILE, 18:24],
                                         op0=ALU.mult, op1=ALU.max))
            link(ve.reciprocal(X[0:TILE, 78:84], X[0:TILE, 66:72]))
            ve.wait_ge(sg["G_ps"], 1)
            ve.tensor_tensor(L[0:TILE], bank[2][0:TILE, 0:384].rearrange("p (i s) -> p i s", i=NT),
                             X[0:TILE, 78:84].unsqueeze(2).broadcast_to([TILE, NT, S]), ALU.mult).then_inc(sg["L_sb"], 1)
            link(ve.reciprocal(X[0:TILE, 60:66], X[0:TILE, 54:60]))
            ve.tensor_tensor(smask[0:TILE], mask_v.unsqueeze(1).broadcast_to([TILE, NT, 3]),
                             X[0:TILE, 60:66].unsqueeze(2).broadcast_to([TILE, NT, 3]), ALU.mult)
            ve.memset(ys[:, :, :, :, :], 0.0)
            nb = (9, 7)
            lt = [bank[3 + q][0:S, 0:T * nb[q]].rearrange("p (b t) -> p b t", b=nb[q]) for q in range(2)]
            le = [LTe[0:S, 324 * q:324 * q + T * nb[q]].rearrange("p (b t) -> p b t", b=nb[q]) for q in range(2)]

            def per_image(o, q):
                return small[0:S, o + 9 * q:o + 9 * q + nb[q]]

            def spread(v, q):
                return v.unsqueeze(2).broadcast_to([S, nb[q], T])

            for q in range(2):
                ve.wait_ge(sg["LT_ps"], q + 1)
                link(ve.tensor_reduce(per_image(0, q), lt[q], AX.X, ALU.max))
                ve.tensor_tensor(le[q], lt[q], spread(per_image(0, q), q), ALU.subtract).then_inc(sg["LT_sub"], 1)
            for q in range(2):
                ve.wait_ge(sg["LT_exp"], q + 1)
                link(ve.tensor_reduce(per_image(30, q), le[q], AX.X, ALU.add))
                link(ve.reciprocal(per_image(50, q), per_image(30, q)))
                ve.tensor_tensor(le[q], le[q], spread(per_image(50, q), q), ALU.mult).then_inc(sg["LT_nrm"], 1)
            for q in range(2):
                ve.wait_ge(sg["D_ps"], q + 1)
                i = slice(3 * q, 3 * q + 3)
                ve.tensor_tensor(Dm[0:TILE, i],
                                 bank[5 - q][0:TILE, 0:192].rearrange("p (i s) -> p i s", i=3).unsqueeze(2).broadcast_to([TILE, 3, 3, S]),
                                 smask[0:TILE, i].unsqueeze(3).broadcast_to([TILE, 3, 3, S]), ALU.mult).then_inc(sg["D_sb"], 1)
            for i in range(NT):
                m = imgs_of(i)
                ve.wait_ge(sg["y_ps"], i + 1)
                ve.tensor_copy(yA[:, :, 3 * i:3 * i + m].rearrange("p s b -> p b s"),
                               bank[6 + i % 2][:, 0:m * S].rearrange("p (b s) -> p b s", b=m)).then_inc(sg["yA_sb"], 1)

            def stationary(g, u):
                ve.tensor_copy(ys[:, u, 0, :, 0:B], yA[:, bass.ds(g * GS, GS), :])
                for e in range(2):
                    p = slice(64 * e, 64 * e + 64)
                    ins = ve.tensor_copy(ys[p, u, 1, e::2, 0:B], yB[p, bass.ds(g * (GS // 2), GS // 2), :])
                ins.then_inc(sg["ys_sb"], 1)

            def hidden(n, u):
                for q in range(2):
                    ve.wait_ge(sg["hT_ps"], 2 * n + (q + 1))
                    ve.tensor_copy(hT[:, u, 3 * q:3 * q + 3, :], bank[2 + q][:, 0:384].rearrange("p (c m) -> p c m", c=3))\
                        .then_inc(sg["hT_sb"], 1)

            def gather(n, r):
                ve.wait_ge(sg["y2_ps"], n + 1)
                ve.tensor_copy(y2[:, r, :], bank[4][:, 0:D]).then_inc(sg["y2_sb"], 1)

            ve.wait_ge(sg["yA_sb"], NT)
            ve.wait_ge(sg["yB_sb"], 2 * NT)
            stationary(0, 0)
            stationary(1, 1)
            link(ve.tensor_reduce(small[0:TILE, 20:26], L[0:TILE], AX.X, ALU.max))
            ve.tensor_tensor(Le[0:TILE], L[0:TILE], small[0:TILE, 20:26].unsqueeze(2).broadcast_to([TILE, NT, S]), ALU.subtract)\
                .then_inc(sg["Lc_sub"], 1)
            ve.wait_ge(sg["Lc_exp"], 1)
            link(ve.tensor_reduce(small[0:TILE, 70:76], Le[0:TILE], AX.X, ALU.add))
            link(ve.reciprocal(small[0:TILE, 80:86], small[0:TILE, 70:76]))
            ve.tensor_tensor(Le[0:TILE], Le[0:TILE], small[0:TILE, 80:86].unsqueeze(2).broadcast_to([TILE, NT, S]), ALU.mult)\
                .then_inc(sg["Lc_nrm"], 1)
            for q in range(2):
                ve.wait_ge(sg["C_ps"], q + 1)
                ve.tensor_copy(C[0:S, 324 * q:324 * q + 324], bank[6 + q][0:S, 0:324]).then_inc(sg["C_sb"], 1)
            for n in range(RING):
                ve.wait_ge(sg["g1_ps"], 2 * n + 2)
                stationary(n + 2, n % 2)
                hidden(n, n % 2)
                gather(n, n)
            with ve.Fori(1, NG // RING - 1) as i:
                for r in range(RING):
                    n = i * RING + r
                    ve.wait_ge(sg["g1_ps"], i * (2 * RING) + (2 * r + 2))
                    stationary(i * RING + (r + 2), r % 2)
                    hidden(n, r % 2)
                    ve.wait_ge(sg["comb_ps"], (i - 1) * RING + (r + 1))
                    gather(n, r)
            for r in range(RING):
                n = NG - RING + r
                if r < 2:
                    ve.wait_ge(sg["g1_ps"], 2 * n + 2)
                    stationary(n + 2, r % 2)
                hidden(n, r % 2)
                ve.wait_ge(sg["comb_ps"], n - RING + 1)
                gather(n, r)

            for q in (0, 2):
                ve.wait_ge(sg["o_ps"], q + 1)
                ve.tensor_copy(h[0:TILE, 2 * q:2 * q + 2, :], bank[5 + q][0:TILE, 0:2 * D].rearrange("p (i d) -> p i d", i=2))\
                    .then_inc(sg["o_sb"], 1)

        @block.tensor
        def _(pe):
            def kr(k):
                return HD + k

            pe.wait_ge(ld_cst, 16)
            pe.wait_ge(ld_wT, 16)
            for q in range(3):
                pe.matmul(bank[q][:, 0:384], dct, wT[:, q * 384:q * 384 + 384], start=True, stop=True).then_inc(sg["weff_ps"], 1)
            pe.wait_ge(ld_mem, 48)
            pe.wait_ge(filled, 1)
            for m in range(2):
                for k in range(2):
                    mm = pe.matmul(bank[5][0:HD, m * M:m * M + M], wM[0:kr(k), k, m * HD:m * HD + HD], memT[0:kr(k), k, :],
                                   start=(k == 0), stop=(k == 1))
            mm.then_inc(sg["mk_ps"], 1)
            for k in range(2):
                mm = pe.matmul(bank[6][0:M, 0:D], memT[0:kr(k), k, :], wM[0:kr(k), k, D:2 * D], start=(k == 0), stop=(k == 1))
            mm.then_inc(sg["mv_ps"], 1)
            pe.wait_ge(ld_x0, 16)
            pe.wait_ge(sg["weff_sb"], 3)

            def xl_transpose(i):
                pe.wait_ge(sg["xl_sb"], i + 1)
                if i >= 2:
                    pe.wait_ge(sg["xlT_sb"], i - 1)
                for k in range(2):
                    mm = pe.transpose(bank[1 + i % 2][0:HD, k * TILE:k * TILE + TILE], xl[0:TILE, i % 2, k * HD:k * HD + HD],
                                      ident[0:TILE, 0:TILE])
                mm.then_inc(sg["xlT_ps"], 1)

            def q_or_k(which, m, n, bk):
                o = which * D + m * HD
                for k in range(2):
                    mm = pe.matmul(bank[bk][0:HD, 0:NHALF], wA[0:kr(k), k, o:o + HD], xlT[0:kr(k), k, n * NHALF:(n + 1) * NHALF],
                                   start=(k == 0), stop=(k == 1))
                mm.then_inc(sg["qk_ps"], 1)

            for i in range(NT):
                r = rows_of(i)
                if i == 2:
                    pe.wait_ge(sg["mk_sb"], 1)
                    pe.wait_ge(sg["mv_sb"], 1)
                if i == 3:
                    pe.wait_ge(ld_x1, 16)
                for c in range(6):
                    mm = pe.matmul(bank[(3 + i) % 8][0:r, 0:D], xT[:, c, i * TILE:i * TILE + r], weff[:, c, :],
                                   start=(c == 0), stop=(c == 5))
                mm.then_inc(sg["h_ps"], 1)
                if i >= 2:
                    xl_transpose(i - 2)
            pe.wait_ge(sg["sl_sb"], 1)
            pe.wait_ge(sg["var_sb"], 4)
            for k in range(2):
                mm = pe.transpose(bank[6][0:HD, k * S:k * S + S], slr[0:S, k * HD:k * HD + HD], ident[0:S, 0:S])
            mm.then_inc(sg["slT_ps"], 1)
            pe.wait_ge(ld_attn, 32)
            pe.wait_ge(filled, 8)
            pe.wait_ge(sg["xlT_sb"], 3)
            q_or_k(1, 0, 0, 3)
            q_or_k(1, 1, 0, 4)
            xl_transpose(NT - 2)
            pe.wait_ge(sg["var_sb"], 5)
            q_or_k(0, 0, 0, 5)
            xl_transpose(NT - 1)
            q_or_k(0, 1, 0, 7)
            pe.wait_ge(sg["xlT_sb"], NT)
            pe.wait_ge(sg["k_sb"], 1)
            q_or_k(1, 0, 1, 3)
            pe.wait_ge(sg["k_sb"], 2)
            q_or_k(1, 1, 1, 4)
            pe.wait_ge(sg["q_sb"], 1)
            q_or_k(0, 0, 1, 5)
            pe.wait_ge(sg["slT_sb"], 1)
            q_or_k(0, 1, 1, 6)

            def alpha(n, m, bk, o):
                c = slice(*CHUNKS[n])
                for k in range(4):
                    src = (aT, a1T)[k // 2]
                    rows = HD + (k == 1)
                    mm = pe.matmul(bank[bk][0:HD, o:o + c.stop - c.start], wAl[0:rows, k, m * HD:m * HD + HD],
                                   src[0:rows, k % 2, c], start=(k == 0), stop=(k == 3))
                return mm

            def project(i):
                r = rows_of(i)
                for k in range(2):
                    mm = pe.matmul(bank[PRB[i]][0:r, 0:D], fT[0:kr(k), k, i * TILE:i * TILE + r], wP[0:kr(k), k, :],
                                   start=(k == 0), stop=(k == 1))
                mm.then_inc(sg["pr_ps"], 1)

            pe.wait_ge(sg["q_sb"], 2)
            for i in range(NT):
                r = rows_of(i)
                if i == 1:
                    pe.wait_ge(sg["q_sb"], 4)
                if i >= 2:
                    pe.wait_ge(sg["v_sb"], i - 1)
                for k in range(2):
                    mm = pe.matmul(bank[7 - i % 2][0:r, 0:D], xlT[0:kr(k), k, i * TILE:i * TILE + r],
                                   wA[0:kr(k), k, 2 * D:3 * D], start=(k == 0), stop=(k == 1))
                mm.then_inc(sg["v_ps"], 1)

            def scores(n):
                pe.wait_ge(sg["kb_sb"], n + 1)
                if n >= 1:
                    pe.wait_ge(sg["p_sub"], n)
                for k in range(2):
                    for e in range(2):
                        b = 2 * n + e
                        mm = pe.matmul(bank[0][64 * e:64 * e + 64, 216 * k:216 * k + 216], qT[0:HD, k, b * T:b * T + 64],
                                       Kb[0:HD, b % 4, k, :], start=True, stop=True)
                mm.then_inc(sg["s_ps"], 1)

            def memory_scores(n):
                i, k = divmod(n, 2)
                r = mrows(i)
                for q in range(2):
                    if n >= 1:
                        pe.wait_ge(sg["p1_exp"], 2 * n - 1 + q)
                    pe.matmul(bank[2 + q][0:r, 0:300], qT[:, k, i * 128:i * 128 + r],
                              MKb[:, k, 300 * q:300 * q + 300], start=True, stop=True).then_inc(sg["s1_ps"], 1)

            pe.wait_ge(sg["var_sb"], NT)
            pe.wait_ge(filled, 9)
            pe.wait_ge(sg["k_sb"], 4)
            scores(0)
            memory_scores(0)
            for n in range(STEPS):
                if 0 < n < NU:
                    memory_scores(n)
                if n + 1 < NB:
                    scores(n + 1)
                if 0 <= n - 1 < NB:
                    u = n - 1
                    pe.wait_ge(sg["p_exp"], u + 1)
                    if u >= 1:
                        pe.wait_ge(sg["pT_sb"], u)
                    for g in range(4):
                        mm = pe.transpose(bank[1][0:TILE, g * 128:g * 128 + 128], Ps[:, u % 2, g * TILE:g * TILE + TILE], ident)
                    mm.then_inc(sg["pT_ps"], 1)
                if 0 <= n - 3 < NU:
                    u = n - 3
                    i, k = divmod(u, 2)
                    r = mrows(i)
                    pe.wait_ge(sg["p1T_sb"], u + 1)
                    if u >= 1:
                        pe.wait_ge(sg["a1T_sb"], u)
                    for par in range(2):
                        for c in range(3):
                            x = 2 * c + par
                            mm = pe.matmul(bank[6][32 * c:32 * c + 32, 0:r], MVz[:, k * HH + x, :], P1T[:, u % 2, x, 0:r],
                                           start=(par == 0), stop=(par == 1))
                    mm.then_inc(sg["a1T_ps"], 1)
                if n >= 3:
                    pe.wait_ge(sg["p1T_sb"], min(n - 2, NU))
                if n >= 4:
                    pe.wait_ge(sg["aT_sb"], min(n - 3, NB))
                if 0 <= n - 3 < NB:
                    u = n - 3
                    pe.wait_ge(sg["a_sb"], u + 1)
                    for k in range(2):
                        mm = pe.transpose(bank[4 + k][0:HD, 384:512], am[:, u % 2, k * HD:k * HD + HD], ident)
                    mm.then_inc(sg["aT_ps"], 1)
                if 0 <= n - 2 < NU:
                    u = n - 2
                    r = mrows(u // 2)
                    pe.wait_ge(sg["p1_norm"], u + 1)
                    for x in range(HH):
                        mm = pe.transpose(bank[4 + x // 3][0:M, (x % 3) * 128:(x % 3) * 128 + r],
                                          P1[0:r, u % 3, x * M:x * M + M], ident[0:r, 0:r])
                    mm.then_inc(sg["p1T_ps"], 1)
                if 0 <= n - 2 < NB:
                    u = n - 2
                    pe.wait_ge(sg["pT_sb"], u + 1)
                    if u == 0:
                        pe.wait_ge(sg["v_sb"], NT)
                    pe.wait_ge(sg["v_mask"], u + 1)
                    if u >= 1:
                        pe.wait_ge(sg["a_sb"], u)
                    for g in range(4):
                        for e in range(2):
                            mm = pe.matmul(bank[7][64 * e:64 * e + 64, g * 48:g * 48 + 48], PT[0:TILE, u % 2, g, 64 * e:64 * e + 64],
                                           Vb[0:TILE, 2 * u + e, g * 48:g * 48 + 48], start=True, stop=True)
                    mm.then_inc(sg["av_ps"], 1)
                if n == NU:
                    pe.wait_ge(ld_late, 80)
                    pe.wait_ge(filled, 10)
                    pe.wait_ge(sg["p_sub"], NB)
                    pe.wait_ge(sg["pT_sb"], NB)
                if n in (NU, NU + 1):
                    m = n - NU
                    alpha(0, m, m, 0).then_inc(sg["al_ps"], 1)
            pe.wait_ge(sg["aT_sb"], NB)
            pe.wait_ge(sg["p1_exp"], 2 * NU)
            for m in range(2):
                alpha(1, m, 2 + m, 0).then_inc(sg["al_ps"], 1)
            pe.wait_ge(sg["a_sb"], NB)
            pe.wait_ge(sg["fT_sb"], 1)
            project(0)
            project(1)
            pe.wait_ge(sg["a1T_sb"], NU)
            alpha(2, 0, 1, 0)
            alpha(2, 1, 1, 256).then_inc(sg["al_ps"], 1)

            def keep_warm(n):
                for _ in range(n):
                    pe.matmul(bank[7][:, 0:NCST], ident, cst[:, :], start=True, stop=True)

            def hn_transpose(i):
                pe.wait_ge(sg["hn_sb"], i + 1)
                if i >= 2:
                    pe.wait_ge(sg["hnT_sb"], i - 1)
                for k in range(2):
                    mm = pe.transpose(bank[i % 2][0:HD, k * TILE:k * TILE + TILE], hn[0:TILE, i, k * HD:k * HD + HD],
                                      ident[0:TILE, 0:TILE])
                mm.then_inc(sg["hnT_ps"], 1)

            def products(i):
                pe.wait_ge(sg["hnT_sb"], i + 1)
                for k in range(2):
                    mm = pe.matmul(bank[2][0:TILE, i * S:i * S + S], hnT[0:HD, k, i * TILE:i * TILE + TILE], slT[0:HD, k, :],
                                   start=(k == 0), stop=(k == 1))
                return mm

            pe.wait_ge(sg["fT_sb"], 2)
            project(2)
            project(3)
            pe.wait_ge(sg["hn_sb"], 2)
            hn_transpose(0)
            pe.wait_ge(sg["fT_sb"], 3)
            project(4)
            project(5)
            hn_transpose(1)
            for i in range(2, NT):
                hn_transpose(i)
                products(i - 2)
            products(NT - 2)
            products(NT - 1).then_inc(sg["G_ps"], 1)
            pe.wait_ge(sg["L_sb"], 1)
            for i in range(NT):
                mm = pe.transpose(bank[3 + i // 3][0:S, (i % 3) * TILE:(i % 3) * TILE + TILE], L[0:TILE, i, :], ident[0:TILE, 0:TILE])
                if i % 3 == 2:
                    mm.then_inc(sg["LT_ps"], 1)
            keep_warm(3)
            pe.wait_ge(filled, 12)
            for i in range(NT):
                pe.wait_ge(sg["LT_nrm"], i // 3 + 1)
                mm = pe.transpose(bank[5 - i // 3][0:TILE, (i % 3) * S:(i % 3) * S + S], LTe[0:S, i * TILE:i * TILE + TILE], ident[0:S, 0:S])
                if i % 3 == 2:
                    mm.then_inc(sg["D_ps"], 1)
            keep_warm(1)
            for i in range(NT):
                m = imgs_of(i)
                pe.wait_ge(sg["D_sb"], i // 3 + 1)
                if i >= 2:
                    pe.wait_ge(sg["yA_sb"], i - 1)
                    pe.wait_ge(sg["yB_sb"], 2 * (i - 1))
                pe.matmul(bank[6 + i % 2][:, 0:m * S], hn[0:TILE, i, 0:128], Dm[0:TILE, i, 0:m, :], start=True, stop=True)
                for e in range(2):
                    mm = pe.matmul(bank[i % 2][64 * e:64 * e + 64, 0:m * S // 2], hn[0:TILE, i, 128:D], Dm[0:TILE, i, 0:m, e::2],
                                   start=True, stop=True)
                mm.then_inc(sg["y_ps"], 1)

            def fc1(n, q, r, u, rounds, first=False):
                if q == 0:
                    pe.wait_ge(sg["ys_sb"], n + 1)
                    pe.wait_ge(ld_b1[r], 16 * rounds)
                    pe.wait_ge(ld_w1[r], 48 * rounds)
                if not first:
                    pe.wait_ge(sg["gelu_sb"], 2 * n + (q - 1))
                cols = slice(q * 384, q * 384 + 384)
                pe.matmul(bank[q][:, 0:384], ind4[r], b1g[r][:, cols], start=True, stop=False, skip_group_check=True)
                for k in range(2):
                    for j in range(GS):
                        w = w1a(r)[:, j, cols] if k == 0 else w1b(r)[:, j // 2, cols]
                        mm = pe.matmul(bank[q][32 * j:32 * j + 32, 0:384], ys[:, u, k, j, :], w, start=False,
                                       stop=(k == 1), skip_group_check=True)
                mm.then_inc(sg["g1_ps"], 1)

            def turn(n, u):
                pe.wait_ge(sg["gelu_sb"], 2 * n + 2)
                for c in range(6):
                    mm = pe.transpose(bank[2 + c // 3][:, (c % 3) * 128:(c % 3) * 128 + 128], hg[:, u, c::6], ident)
                    if c % 3 == 2:
                        mm.then_inc(sg["hT_ps"], 1)

            def fc2(n, r, u, rounds, first=False, last=False):
                pe.wait_ge(ld_w2[r], 16 * rounds)
                if not first:
                    pe.wait_ge(sg["y2_sb"], n)
                for c in range(6):
                    if c % 3 == 0:
                        pe.wait_ge(sg["hT_sb"], 2 * n + (c // 3 + 1))
                    if last and c == 3:
                        pe.wait_ge(ld_w2_end, 16)
                    for j in range(GS):
                        mm = pe.matmul(bank[4][32 * j:32 * j + 32, 0:D], hT[:, u, c, 32 * j:32 * j + 32], w2r(r)[:, j, c, :],
                                       start=(c == 0), stop=(c == 5))
                mm.then_inc(sg["y2_ps"], 1)

            pe.wait_ge(sg["yA_sb"], NT)
            keep_warm(1)
            fc1(0, 0, 0, 0, 1, first=True)
            fc1(0, 1, 0, 0, 1, first=True)
            pe.wait_ge(sg["Lc_nrm"], 1)
            pe.wait_ge(sg["yA_sb"], NT)
            for i in range(NT):
                mm = pe.transpose(bank[6 + i // 3][0:S, (i % 3) * TILE:(i % 3) * TILE + TILE], Le[0:TILE, i, :], ident[0:TILE, 0:TILE])
                if i % 3 == 2:
                    mm.then_inc(sg["C_ps"], 1)

            def start_sums():
                pe.wait_ge(sg["C_sb"], 2)
                for q in range(NT // 2):
                    pe.matmul(bank[5 + q][0:TILE, 0:2 * D], ident[0:TILE, 0:TILE], h[0:TILE, 2 * q:2 * q + 2, :], start=True, stop=False,
                              skip_group_check=True)
                for i in range(NT):
                    pe.matmul(total(i), C[0:S, i * TILE:i * TILE + rows_of(i)], b2s[0:S, :], start=False, stop=False,
                              skip_group_check=True)

            def combine(n, r, last=False):
                pe.wait_ge(sg["cbd_sb"], n + 1)
                pe.wait_ge(sg["y2_sb"], n + 1)
                for i in range(NT):
                    mm = pe.matmul(total(i), Cbd[:, r % 2, i * TILE:i * TILE + rows_of(i)], y2[:, r, :], start=False, stop=last,
                                   skip_group_check=True)
                    if last and i % 2 == 1:
                        mm.then_inc(sg["o_ps"], 1)
                if not last:
                    mm.then_inc(sg["comb_ps"], 1)

            def step(n, r, i, first=False):
                q = r + 1
                rounds = i + (q // RING + 1)
                fc1(n, 0, q % RING, q % 2, rounds)
                turn(n - 1, r % 2)
                fc1(n, 1, q % RING, q % 2, rounds)
                if not first:
                    combine(n - 2, (r - 1) % RING)
                fc2(n - 1, r, r % 2, i + 1, first=first)

            for r in range(RING):
                if r == RING - 1:
                    pe.wait_ge(ld_w1_start, 48)
                step(r + 1, r, 0, first=(r == 0))
                if r == 0:
                    start_sums()
            with pe.Fori(1, NG // RING - 1) as i:
                for r in range(RING):
                    step(i * RING + (r + 1), r, i)
            i = NG // RING - 1
            for r in range(RING - 2):
                step(i * RING + r + 1, r, i)
            n, u = NG - 1, (NG - 1) % 2
            turn(n - 1, 1 - u)
            combine(n - 2, RING - 3)
            for q in range(2):
                fc1(n, q, RING - 1, u, NG // RING)
            pe.wait_ge(sg["hT_sb"], 2 * n)
            turn(n, u)
            fc2(n - 1, RING - 2, 1 - u, NG // RING)
            combine(n - 1, RING - 2)
            fc2(n, RING - 1, u, NG // RING, last=True)
            combine(n, RING - 1, last=True)


_ORDER = ["xT", "wT", "cst", "L0_tok_b", "L0_attn_w_attn", "L0_attn_b_attn", "L0_attn_w_proj", "L0_attn_b_proj",
          "L0_attn_w_mem", "L0_attn_b_mem", "L0_attn_w_alpha", "L0_attn_b_alpha", "memT", "L0_ffn_slots",
          "L0_ffn_scale", "L0_ffn_fc1_weight", "L0_ffn_fc1_bias", "L0_ffn_fc2_weight", "L0_ffn_fc2_bias",
          "L0_ffn_norm_weight"]


def constants():
    n = np.arange(8)
    dct = np.sqrt(2.0 / 8) * np.cos(np.pi * (2 * n[None, :] + 1) * n[:, None] / 16)
    dct[0] /= np.sqrt(2.0)
    p = np.arange(128)
    c = np.zeros((128, NCST), np.float32)
    c[:, C_ID:C_ID + 128] = np.eye(128)
    c[:, C_G:C_G + 128] = np.kron(dct, np.kron(np.eye(2), dct))
    for o in (0, 64):
        c[o:o + GS, C_IND:C_IND + 128] = p[None, :] // 32 == np.arange(GS)[:, None]
    c[:, C_MK:C_MK + HH] = p[:, None] // DH == np.arange(HH)[None, :]
    c[:, C_MV:C_MV + 3] = p[:, None] // T == np.arange(3)[None, :]
    c[:, C_MB:C_MB + B] = p[:, None] % BP == np.arange(B)[None, :]
    return c


def kernel(**inputs):
    import concourse.bacc as bacc
    from concourse.bass_utils import run_bass_kernel_spmd

    a = {k: np.asarray(v) for k, v in inputs.items()}
    a["xT"] = a["x"].reshape(B, 3, 6, 2, 8, 6, 16).transpose(4, 6, 1, 3, 0, 2, 5).reshape(128, 6 * NTOK)
    a["wT"] = a["L0_tok_w"].reshape(D, 3, 2, 8, 16).transpose(3, 4, 1, 2, 0).reshape(128, 6 * D)
    a["memT"] = a["L0_attn_memory_features"][0].T
    a["cst"] = constants()
    nc = bacc.Bacc("TRN2", target_bir_lowering=False, num_devices=1)
    arrays, args = {}, []
    for name in _ORDER:
        v = np.ascontiguousarray(a[name])
        arrays[f"in_{name}"] = v
        args.append(nc.dram_tensor(f"in_{name}", v.shape, mybir.dt.from_np(v.dtype), kind="ExternalInput").ap())
    args.append(nc.dram_tensor("out_0", (B, T, D), F32, kind="ExternalOutput").ap())
    vit_tower(nc, *args)
    return run_bass_kernel_spmd(nc, [arrays], core_ids=[0]).results[0]["out_0"]
```
